# Optimizing a Trainium2 kernel written in Bass

```python
import numpy as np
import jax
import jax.numpy as jnp

def _softmax(x, axis=-1):
    return jax.nn.softmax(x, axis=axis)

def _gelu(x):
    return jax.nn.gelu(x, approximate=True)

def _silu(x):
    return jax.nn.silu(x)

def _sigmoid(x):
    return jax.nn.sigmoid(x)

def _layernorm(x, axis=-1, eps=1e-05):
    m = jnp.mean(x, axis=axis, keepdims=True)
    v = jnp.var(x, axis=axis, keepdims=True)
    return (x - m) / jnp.sqrt(v + eps)

def _scatter_add(tgt, idx, src, axis=0):
    return tgt.at[idx].add(src)

def _segment_sum(src, seg, n):
    return jax.ops.segment_sum(src, seg, n)
kernel_name = 'mk_flamingo_gated_d1_seqx_r4_7e94e8'

def setup_inputs(seed: int=0):
    np.random.seed(seed)
    _w = jnp.asarray

    def _rec_inputs():
        import jax
        import jax.numpy as jnp
        _rk = jax.random.key(seed)
        x = 7.22e-05 + 1 * jax.random.normal(jax.random.fold_in(_rk, 1), (4, 512, 512), jnp.float32)
        _lenS = 512 - jax.random.randint(jax.random.fold_in(_rk, 7), (4,), 0, max(1, 512 // 4) + 1, jnp.int32)
        _lenS2 = 512 - jax.random.randint(jax.random.fold_in(_rk, 8), (4,), 0, max(1, 512 // 4) + 1, jnp.int32)
        _ctx_1024P = jax.random.normal(jax.random.fold_in(_rk, 11), (4, 16, 256), jnp.float32)
        _ctx_1024c = jax.random.dirichlet(jax.random.fold_in(_rk, 511), 0.3 * jnp.ones((16,), jnp.float32), (4, 512))
        _ctx_1024t = jnp.einsum('bsk,bkd->bsd', _ctx_1024c, _ctx_1024P)
        _ctx_1024t = _ctx_1024t * jax.lax.rsqrt(jnp.mean(jnp.square(_ctx_1024t)) + 1e-12) * 0.953939
        ctx_1024 = 2.81802e-05 + 1.00001 * (_ctx_1024t + 0.3 * jax.random.normal(jax.random.fold_in(_rk, 611), (4, 512, 256), jnp.float32))
        _g = jax.random.normal(jax.random.fold_in(_rk, 9001), (2, 1), jnp.float32)
        _g = jnp.sign(_g) * jnp.maximum(jnp.abs(_g), 1.0) + (_g == 0) * 1.0
        g_xattn = _g[0]
        g_ffn = _g[1]
        return (x, ctx_1024, g_xattn, g_ffn)
    x, ctx_1024, g_xattn, g_ffn = _rec_inputs()

    def _L0_xattn_setup():
        import jax, jax.numpy as jnp
        import numpy as np
        key = jax.random.key(seed)
        ks = jax.random.split(key, 6)
        B, L, N, C, D = (8, 128, 512, 256, 128)
        return {'teacher_logits': jax.random.normal(ks[0], (B, L, N), dtype=jnp.float32), 'teacher_features': jax.random.normal(ks[1], (B, N, C), dtype=jnp.float32), 'Wq': jax.random.normal(ks[2], (D, C), dtype=jnp.float32) * (1.0 / np.sqrt(C)), 'bq': jnp.zeros((D,), dtype=jnp.float32), 'Wk': jax.random.normal(ks[3], (D, C), dtype=jnp.float32) * (1.0 / np.sqrt(C)), 'bk': jnp.zeros((D,), dtype=jnp.float32)}
    _L0_xattn_all = _L0_xattn_setup()
    _L0_xattn_in = {k: v for k, v in _L0_xattn_all.items() if k in ('Wq', 'bq', 'Wk', 'bk')}
    del _L0_xattn_all

    def _L0_ffn_setup():
        import jax, jax.numpy as jnp
        import numpy as np
        HIDDEN = 512
        INTER = 1408
        B, S = (2, 512)

        def _ternary(key, shape):
            return jax.random.randint(key, shape, -1, 2).astype(jnp.float32)
        key = jax.random.key(seed)
        ks = jax.random.split(key, 7)
        x = jax.random.normal(ks[0], (B, S, HIDDEN), dtype=jnp.float32)
        gate_w = _ternary(ks[1], (INTER, HIDDEN))
        up_w = _ternary(ks[2], (INTER, HIDDEN))
        down_w = _ternary(ks[3], (HIDDEN, INTER))
        gate_s = jax.random.uniform(ks[4], (INTER,), minval=0.01, maxval=0.1, dtype=jnp.float32)
        up_s = jax.random.uniform(ks[5], (INTER,), minval=0.01, maxval=0.1, dtype=jnp.float32)
        down_s = jax.random.uniform(ks[6], (HIDDEN,), minval=0.01, maxval=0.1, dtype=jnp.float32)
        return {'x': x, 'gate_w': gate_w, 'up_w': up_w, 'down_w': down_w, 'gate_s': gate_s, 'up_s': up_s, 'down_s': down_s}
    _L0_ffn_all = _L0_ffn_setup()
    _L0_ffn_in = {k: v for k, v in _L0_ffn_all.items() if k in ('gate_w', 'up_w', 'down_w', 'gate_s', 'up_s', 'down_s')}
    del _L0_ffn_all
    return {'x': x, 'ctx_1024': ctx_1024, 'g_xattn': g_xattn, 'g_ffn': g_ffn, 'L0_xattn_Wq': _L0_xattn_in['Wq'], 'L0_xattn_bq': _L0_xattn_in['bq'], 'L0_xattn_Wk': _L0_xattn_in['Wk'], 'L0_xattn_bk': _L0_xattn_in['bk'], 'L0_ffn_gate_w': _L0_ffn_in['gate_w'], 'L0_ffn_up_w': _L0_ffn_in['up_w'], 'L0_ffn_down_w': _L0_ffn_in['down_w'], 'L0_ffn_gate_s': _L0_ffn_in['gate_s'], 'L0_ffn_up_s': _L0_ffn_in['up_s'], 'L0_ffn_down_s': _L0_ffn_in['down_s']}

def reference(x, ctx_1024, g_xattn, g_ffn, L0_xattn_Wq, L0_xattn_bq, L0_xattn_Wk, L0_xattn_bk, L0_ffn_gate_w, L0_ffn_up_w, L0_ffn_down_w, L0_ffn_gate_s, L0_ffn_up_s, L0_ffn_down_s):
    import jax
    import jax.numpy as jnp

    def _L0_xattn_ref(teacher_logits, teacher_features, Wq, bq, Wk, bk):
        import jax, jax.numpy as jnp
        import numpy as np
        query = jnp.einsum('bnc,dc->bnd', teacher_features, Wq) + bq
        key = jnp.einsum('bnc,dc->bnd', teacher_features, Wk) + bk
        energy = jnp.einsum('bnd,bmd->bnm', query, key)
        attention = jax.nn.softmax(energy, axis=-1)
        x_m = jnp.einsum('bln,bmn->blm', teacher_logits, attention)
        return x_m

    def _L0_ffn_ref(x, gate_w, up_w, down_w, gate_s, up_s, down_s):
        import jax, jax.numpy as jnp
        import numpy as np
        HIDDEN = 512
        INTER = 1408
        B, S = (2, 512)

        def _ternary(key, shape):
            return jax.random.randint(key, shape, -1, 2).astype(jnp.float32)
        b, s, h = x.shape
        xf = x.reshape(b * s, h)
        g = jnp.einsum('th,ih->ti', xf, gate_w) * gate_s
        u = jnp.einsum('th,ih->ti', xf, up_w) * up_s
        hdn = jax.nn.silu(g) * u
        out = jnp.einsum('ti,hi->th', hdn, down_w) * down_s
        return out.reshape(b, s, -1)
    x = x + jnp.tanh(g_xattn[0]) * _L0_xattn_ref(_layernorm(x, axis=-1), ctx_1024, L0_xattn_Wq, L0_xattn_bq, L0_xattn_Wk, L0_xattn_bk)
    x = x + jnp.tanh(g_ffn[0]) * _L0_ffn_ref(_layernorm(x, axis=-1), L0_ffn_gate_w, L0_ffn_up_w, L0_ffn_down_w, L0_ffn_gate_s, L0_ffn_up_s, L0_ffn_down_s)
    return x

_drawn_inputs = setup_inputs


def setup_inputs(seed=0):
    import zlib

    import numpy as np

    out = dict(_drawn_inputs(seed))
    spreads = {'L0_xattn_bq': (0.0, 0.1), 'L0_xattn_bk': (0.0, 0.1)}
    factors = {}
    for name, (base, spread) in spreads.items():
        noise = np.random.default_rng([zlib.crc32(name.encode()), seed]).standard_normal(out[name].shape)
        drawn = base * np.exp(spread * noise) if base else spread * noise
        out[name] = jnp.asarray(drawn.astype(out[name].dtype))
    for name, factor in factors.items():
        out[name] = (out[name] * factor).astype(out[name].dtype)
    return out
```

```python
import concourse.bass as bass
from concourse import mybir
from concourse.alu_op_type import AluOpType as ALU
from contextlib import ExitStack

P = 128
B, S, C, D, F = 4, 512, 256, 128, 1408
T = S // P
CT = C // P
NU = F // P
WCH = T * F // B
EPS = 1e-5
HI, LO = 0, 1
Q, K = 0, 1
GATE, UP, DOWN = 0, 1, 2
W3 = 3
DMA = 16

EVENTS = [("unit", 1), ("unit", 2), ("unit", 3), ("unit", 4), ("unit", 5), ("turn", (0, 1)),
          ("unit", 6), ("turn", (2,)), ("unit", 7), ("turn", (3,)), ("unit", 8), ("unit", 9), ("unit", 10),
          ("unit", NU)]
LAST_EVENTS = [e for e in EVENTS if e[0] == "unit" and e[1] < NU]
NE = len(EVENTS)
NTURN = sum(e[0] == "turn" for e in EVENTS)
STATS_AFTER, NORM_AFTER = 2, 4


def flamingo_kernel(nc, x, xT, ctxT, wqk, bqk, gates, w3, scales, down_s, out):
    f32, f32r, i32 = mybir.dt.float32, mybir.dt.float32r, mybir.dt.int32
    ACT = mybir.ActivationFunctionType
    AX = mybir.AxisListType
    ds = bass.ds

    x_rows = x.rearrange("b (t p) n -> b p t n", p=P)
    out_rows = out.rearrange("b (t p) n -> b p t n", p=P)
    xT_rows = xT.rearrange("b (k p) l -> b p k l", p=P)
    ctxT_rows = ctxT.rearrange("b (c p) s -> b p c s", p=P)

    with ExitStack() as stack:
        def sb(name, shape, dt=f32):
            return stack.enter_context(nc.sbuf_tensor(name, shape, dt))

        def sem(name):
            return stack.enter_context(nc.semaphore(name))

        X = sb("X", [P, B * T, S])
        Whi = sb("Whi", [P, W3, T * F], f32r)
        wraw = sb("wraw", [P, W3, WCH])
        actT = sb("actT", [P, 2, 2, T, S], f32r)
        mixT = sb("mixT", [P, 2, T, S], f32r)
        work = sb("work", [P, T, S])
        xraw = sb("xraw", [P, T, S])
        craw = sb("craw", [P, CT, S])
        csp = sb("csp", [P, 2, CT, S], f32r)
        qks = sb("qks", [P, 2, 2, S], f32r)
        wqs = sb("wqs", [P, 2, 2, CT, D], f32r)
        dsb = sb("dsb", [P, S])
        ident = sb("ident", [P, P])
        ones = sb("ones", [P, 1])
        half = sb("half", [P, T])
        zero = sb("zero", [P, 1])
        start = sb("start", [P, 2])
        epst = sb("epst", [P, T])
        bias = sb("bias", [P, 2])
        g2 = sb("g2", [P, 2])
        tg = sb("tg", [P, 2])
        usc = sb("usc", [P, 2, NU])
        st = sb("st", [P, T, 6])
        mv = sb("mv", [P, T, 2])
        ve = sb("ve", [P, T])
        rs = sb("rs", [P, T])
        ms = sb("ms", [P, T])
        s1 = sb("s1", [P, B * T])
        nb = sb("nb", [P, B * T])
        nmax = sb("nmax", [P, T])
        rsum = sb("rsum", [P, T])
        rinv = sb("rinv", [P, T])
        odd = sb("odd", [P, W3 * B])
        oddp = sb("oddp", [P, 1])
        flag = sb("flag", [1, 1], i32)
        wqraw = work[:, 0, :]
        hid = work[:, 2:4, :]
        scaled = work[:, 0:2, :]
        wlo_gu = csp[:, :, :, :].rearrange("p a c s -> p (a c s)")
        wlo_dn = qks[:, :, :, :].rearrange("p a c s -> p (a c s)")
        actf = actT[:, :, :, :, :].rearrange("p e a k s -> p (e a k s)")
        Xf = X[:, :, :].rearrange("p t n -> p (t n)")

        def fl(ap):
            return ap.bitcast(f32)

        sc = stack.enter_context(nc.psum_tensor("sc", [P, T, S], f32))
        slot = stack.enter_context(nc.psum_tensor("slot", [P, 2, 2, S], f32))

        ctx_in, wqk_in, small_in, xt_in, x_in, const_in = (sem(n) for n in (
            "ctx_in", "wqk_in", "small_in", "xt_in", "x_in", "const_in"))
        w_in = [sem(f"w_in{m}") for m in range(W3)]
        ident_set, ident_ready = sem("ident_set"), sem("ident_ready")
        wqk_hi, wqk_lo, ctx_hi, ctx_lo = sem("wqk_hi"), sem("wqk_lo"), sem("ctx_hi"), sem("ctx_lo")
        proj_done, qk_hi, qk_lo = sem("proj_done"), sem("qk_hi"), sem("qk_lo")
        score_done, max_ready, exp_done, inv_ready, attn_ready = (sem(n) for n in (
            "score_done", "max_ready", "exp_done", "inv_ready", "attn_ready"))
        turned, turned_hi, turned_lo = sem("turned"), sem("turned_hi"), sem("turned_lo")
        xt_hi, xt_lo = sem("xt_hi"), sem("xt_lo")
        stats_raw, stats_ready, pool_step, scale_ready, tanh_ready = (sem(n) for n in (
            "stats_raw", "stats_ready", "pool_step", "scale_ready", "tanh_ready"))
        xt_scaled, const_set = sem("xt_scaled"), sem("const_set")
        shifted, mix_done, mix_free = sem("shifted"), sem("mix_done"), sem("mix_free")
        w_hi, w_checked, odd_summed, odd_total, flag_ready, dsb_ready = (sem(n) for n in (
            "w_hi", "w_checked", "odd_summed", "odd_total", "flag_ready", "dsb_ready"))
        stats2_raw, stats2_ready, rstd2_ready, normed = (sem(n) for n in (
            "stats2_raw", "stats2_ready", "rstd2_ready", "normed"))
        slot_ready, slot_free, silu_done, hid_hi, hid_lo, down_done = (sem(n) for n in (
            "slot_ready", "slot_free", "silu_done", "hid_hi", "hid_lo", "down_done"))
        out_free, scaled_ready, y_ready, y_out = sem("out_free"), sem("scaled_ready"), sem("y_ready"), sem("y_out")
        raw_in, wlo_gu_ready, wlo_dn_ready = sem("raw_in"), sem("wlo_gu_ready"), sem("wlo_dn_ready")

        block = stack.enter_context(nc.Block())

        def by_weights(eng, program):
            eng.wait_ge(flag_ready, 1)
            some = eng.value_load(flag[0:1, 0:1], min_val=0, max_val=1)
            with eng.If(some > 0):
                program(True)
            with eng.Else():
                program(False)

        def events(b, last):
            for j, (kind, what) in enumerate(LAST_EVENTS if last else EVENTS):
                yield kind, what, b * NE + 1 + j, (1 + j) % 2

        @block.sync
        def _(sp):
            def load_piece(m, b):
                sp.dma_start(wraw[:, m, :], w3[m, :, ds(b * WCH, WCH)]).then_inc(w_in[m], DMA)

            sp.dma_start(craw[:, :, :], ctxT_rows[0]).then_inc(ctx_in, DMA)
            sp.dma_start(wqraw.rearrange("p (m c d) -> p m c d", m=2, c=CT),
                         wqk.rearrange("m (c p) d -> p m c d", p=P)).then_inc(wqk_in, DMA)
            sp.dma_start(bias[:, :], bqk).then_inc(small_in, DMA)
            sp.dma_start(g2[:, :], gates.partition_broadcast(P)).then_inc(small_in, DMA)
            sp.dma_start(xraw[:, :, :], xT_rows[0]).then_inc(xt_in, DMA)
            sp.dma_start(X[:, 0:T, :], x_rows[0]).then_inc(x_in, DMA)
            sp.dma_start(usc[:, :, :].rearrange("p a u -> p (a u)"), scales).then_inc(const_in, DMA)
            sp.dma_start(dsb[:, :], down_s.partition_broadcast(P)).then_inc(const_in, DMA)
            for m in range(W3):
                load_piece(m, 0)
            with sp.Fori(0, B - 1) as b:
                sp.wait_ge(ctx_lo, b + 1)
                sp.dma_start(craw[:, :, :], ctxT_rows[ds(b + 1, 1)].rearrange("o p c s -> (o p) c s")).then_inc(ctx_in, DMA)
                sp.wait_ge(x_in, (b + 1) * DMA)
                sp.dma_start(Xf[:, ds((b + 1) * (T * S), T * S)].rearrange("p (t n) -> p t n", n=S),
                             x_rows[ds(b + 1, 1)].rearrange("o p t n -> (o p) t n")).then_inc(x_in, DMA)
                sp.wait_ge(xt_lo, (b + 1) * T)
                sp.dma_start(xraw[:, :, :], xT_rows[ds(b + 1, 1)].rearrange("o p k l -> (o p) k l")).then_inc(xt_in, DMA)
                for m in range(W3):
                    sp.wait_ge(w_checked, b * W3 + m + 1)
                    load_piece(m, b + 1)

            def phase_b(general):
                def raw_weights(b, i):
                    u, c = b * NU + i, (i % NU) * P
                    if not isinstance(b, int) or u > 0:
                        sp.wait_ge(wlo_dn_ready, u)
                    for m in (GATE, UP):
                        sp.dma_start(wraw[:, m, 0:T * P].rearrange("p (k c) -> p k c", c=P),
                                     w3[m].rearrange("p (k f) -> p k f", f=F)[:, :, c:c + P]).then_inc(raw_in, DMA)
                    sp.dma_start(wraw[:, DOWN, 0:S], w3[DOWN, :, (i % NU) * S:(i % NU + 1) * S]).then_inc(raw_in, DMA)

                def batch(b, last):
                    if general:
                        for kind, i, _, _ in events(b, last):
                            if kind == "unit":
                                raw_weights(b, i)
                    if not last:
                        sp.wait_ge(y_ready, (b + 1) * T)
                        sp.dma_start(out_rows[ds(b, 1)].rearrange("o p t n -> (o p) t n"),
                                     Xf[:, ds(b * (T * S), T * S)].rearrange("p (t n) -> p t n", n=S)).then_inc(y_out, DMA)
                    else:
                        for t in range(T):
                            sp.wait_ge(y_ready, b * T + t + 1)
                            sp.dma_start(out_rows[b][:, t, :], X[:, b * T + t, :]).then_inc(y_out, DMA)

                if general:
                    raw_weights(0, 0)
                with sp.Fori(0, B - 1) as b:
                    batch(b, False)
                batch(B - 1, True)
                sp.wait_ge(y_out, (B - 1 + T) * DMA)

            by_weights(sp, phase_b)

        @block.tensor
        def _(pe):
            MM = nc.tensor.matmul

            def project(b):
                pe.wait_ge(ctx_lo, b + 1)
                for m in (Q, K):
                    steps = [(wp, cp, c) for c in range(CT) for wp, cp in ((HI, HI), (LO, HI), (HI, LO))]
                    for n, (wp, cp, c) in enumerate(steps):
                        last = MM(slot[:, 0, m, :], wqs[:, wp, m, c, :], csp[:, cp, c, :],
                                  start=(n == 0), stop=(n == len(steps) - 1))
                    last.then_inc(proj_done, 1)

            def scores(b):
                pe.wait_ge(qk_lo, 2 * b + 2)
                for t in range(T):
                    for n, (qp, kp) in enumerate(((HI, HI), (LO, HI), (HI, LO))):
                        last = MM(sc[:, t, :], qks[:, qp, Q, t * P:(t + 1) * P], qks[:, kp, K, :],
                                  start=(n == 0), stop=(n == 2))
                    last.then_inc(score_done, 1)

            def turn(bank, src, k):
                for t in range(T):
                    last = nc.tensor.transpose(bank[:, t * P:(t + 1) * P], src[:, t, k * P:(k + 1) * P], ident[:, :])
                return last

            def turn_attention(b):
                pe.wait_ge(attn_ready, (b + 1) * T)
                for k in range(T):
                    last = turn(sc[:, k, :], work, k)
                    if k % 2:
                        last.then_inc(turned, 1)

            def mix(b, t):
                pe.wait_ge(mix_free, b * T + t + 1)
                pe.wait_ge(xt_lo, b * T + t + 1)
                steps = [(k, xp, ap) for k in range(T) for xp, ap in ((HI, HI), (LO, HI), (HI, LO))]
                for n, (k, xp, ap) in enumerate(steps):
                    if t == 0 and n % 6 == 0:
                        pe.wait_ge(turned_lo, 2 * b + k // 2 + 1)
                    last = MM(slot[:, 1, t % 2, :], actT[:, 0, xp, k, t * P:(t + 1) * P], mixT[:, ap, k, :],
                              start=(n == 0), stop=(n == len(steps) - 1))
                last.then_inc(mix_done, 1)

            pe.wait_ge(wqk_lo, 1)
            project(0)
            scores(0)
            pe.wait_ge(ident_ready, 2)
            with pe.Fori(0, B - 1) as b:
                turn_attention(b)
                project(b + 1)
                mix(b, 0)
                scores(b + 1)
                for t in range(1, T):
                    mix(b, t)
            turn_attention(B - 1)
            mix(B - 1, 0)
            mix(B - 1, 1)
            pe.wait_ge(normed, T)
            for k in range(T):
                last = turn(sc[:, k, :], xraw, k)
                if k % 2:
                    last.then_inc(turned, 1)
            mix(B - 1, 2)
            mix(B - 1, 3)
            pe.wait_ge(odd_summed, 1)
            MM(slot[0:1, 0, 0, 0:1], oddp[:, 0:1], ones[:, 0:1], start=True, stop=True).then_inc(odd_total, 1)

            def phase_b(general):
                parts = ((HI, HI), (HI, LO), (LO, HI))[:3 if general else 2]

                def gate_up(b, i, s):
                    c, buf = (i % NU) * P, (b + 1 + i // NU) % 2
                    if general:
                        pe.wait_ge(wlo_gu_ready, b * NU + i + 1)
                    for m in (GATE, UP):
                        steps = [(k, wp, ap) for k in range(T) for wp, ap in parts]
                        for n, (k, wp, ap) in enumerate(steps):
                            w = Whi[:, m, k * F + c:k * F + c + P] if wp == HI else wlo_gu[:, (m * T + k) * P:(m * T + k + 1) * P]
                            last = MM(slot[:, s, m, :], w, actf[:, ds(buf * (2 * T * S) + (ap * T + k) * S, S)],
                                      start=(n == 0), stop=(n == len(steps) - 1))
                    last.then_inc(slot_ready, 1)

                def down(b, i):
                    pe.wait_ge(hid_lo, b * NU + i + 1)
                    if general:
                        pe.wait_ge(wlo_dn_ready, b * NU + i + 1)
                    for t in range(T):
                        if i == 0:
                            pe.wait_ge(out_free, b * T + t + 1)
                        for n, (wp, hp) in enumerate(parts):
                            w = Whi[:, DOWN, i * S:(i + 1) * S] if wp == HI else wlo_dn[:, 0:S]
                            last = MM(sc[:, t, :], mixT[:, hp, i % T, t * P:(t + 1) * P], w,
                                      start=(i == 0 and n == 0), stop=(i == NU - 1 and n == len(parts) - 1))
                    last.then_inc(down_done, 1)

                def batch(b, last):
                    for kind, what, e, s in events(b, last):
                        pe.wait_ge(slot_free, e + 1)
                        if kind == "unit":
                            gate_up(b, what, s)
                            down(b, what - 1)
                        else:
                            for n, k in enumerate(what):
                                if k == 0:
                                    pe.wait_ge(normed, (b + 2) * T)
                                turned_now = turn(slot[:, s, n, :], xraw, k)
                            turned_now.then_inc(slot_ready, 1)
                    if last:
                        down(b, NU - 1)

                pe.wait_ge(out_free, T)
                gate_up(0, 0, 0)
                pe.wait_ge(mix_free, B * T + 2)
                with pe.Fori(0, B - 1) as b:
                    batch(b, False)
                batch(B - 1, True)

            by_weights(pe, phase_b)

        @block.scalar
        def _(act):
            A = nc.scalar.activation

            def context_hi(b):
                act.wait_ge(ctx_in, (b + 1) * DMA)
                if not isinstance(b, int):
                    act.wait_ge(proj_done, 2 * b)
                A(csp[:, HI, :, :], craw[:, :, :], ACT.Copy).then_inc(ctx_hi, 1)

            def project_hi(b):
                for m in (Q, K):
                    act.wait_ge(proj_done, 2 * b + m + 1)
                    A(qks[:, HI, m, :], slot[:, 0, m, :], ACT.Identity, bias=bias[:, m:m + 1]).then_inc(qk_hi, 1)

            def softmax_exp(b):
                for t in range(T):
                    act.wait_ge(max_ready, 2 * b + t // 2 + 1)
                    A(work[:, t, :], sc[:, t, :], ACT.Exp, bias=nmax[:, t:t + 1],
                      accum_out=rsum[:, t:t + 1]).then_inc(exp_done, 1)

            def turned_hi_half(b, h, dst):
                act.wait_ge(turned, 2 * b + h + 1)
                A(dst[:, 2 * h:2 * h + 2, :], sc[:, 2 * h:2 * h + 2, :], ACT.Copy).then_inc(turned_hi, 1)

            def shift(b):
                act.wait_ge(scale_ready, b + 1)
                for t in range(T):
                    row = Xf[:, ds(b * (T * S) + t * S, S)]
                    A(row, row, ACT.Identity, bias=nb[:, ds(b * T + t, 1)]).then_inc(shifted, 1)

            def weights_hi(b, m):
                act.wait_ge(w_in[m], (b + 1) * DMA)
                A(Whi[:, m, ds(b * WCH, WCH)], wraw[:, m, :], ACT.Copy).then_inc(w_hi, 1)

            act.wait_ge(wqk_in, DMA)
            A(wqs[:, HI, :, :, :].rearrange("p m c d -> p (m c d)"), wqraw, ACT.Copy).then_inc(wqk_hi, 1)
            context_hi(0)
            act.wait_ge(small_in, 2 * DMA)
            A(tg[:, :], g2[:, :], ACT.Tanh).then_inc(tanh_ready, 1)
            project_hi(0)
            softmax_exp(0)
            with act.Fori(0, B - 1) as b:
                context_hi(b + 1)
                for h in range(2):
                    turned_hi_half(b, h, mixT[:, HI])
                project_hi(b + 1)
                shift(b)
                weights_hi(b, GATE)
                softmax_exp(b + 1)
                weights_hi(b, UP)
                weights_hi(b, DOWN)
            for h in range(2):
                turned_hi_half(B - 1, h, mixT[:, HI])
            shift(B - 1)
            for m in range(W3):
                weights_hi(B - 1, m)
            for h in range(2):
                turned_hi_half(B, h, actT[:, 1, HI])

            def phase_b(general):
                def unit(b, i, e, s):
                    act.wait_ge(slot_ready, e + 1)
                    A(craw[:, s, :], slot[:, s, GATE, :], ACT.Silu, scale=usc[:, GATE, i % NU:i % NU + 1]).then_inc(silu_done, 1)
                    act.wait_ge(slot_free, e + 3)
                    A(mixT[:, HI, (i % NU) % T, :], hid[:, s, :], ACT.Copy).then_inc(hid_hi, 1)

                def batch(b, last):
                    for kind, what, e, s in events(b, last):
                        if kind == "unit":
                            unit(b, what, e, s)
                        else:
                            act.wait_ge(slot_ready, e + 1)
                            A(actf[:, ds((b % 2) * (2 * T * S) + (HI * T + what[0]) * S, len(what) * S)],
                              slot[:, s, 0:len(what), :].rearrange("p k s -> p (k s)"), ACT.Copy).then_inc(turned_hi, 1)

                unit(0, 0, 0, 0)
                with act.Fori(0, B - 1) as b:
                    batch(b, False)
                batch(B - 1, True)

            by_weights(act, phase_b)

        @block.vector
        def _(dve):
            V = nc.vector
            steps_done = [0]

            def context_lo(b):
                dve.wait_ge(ctx_hi, b + 1)
                V.tensor_tensor(csp[:, LO, :, :], craw[:, :, :], fl(csp[:, HI, :, :]), ALU.subtract).then_inc(ctx_lo, 1)

            def project_lo(b):
                for m in (Q, K):
                    dve.wait_ge(qk_hi, 2 * b + m + 1)
                    V.scalar_tensor_tensor(out=qks[:, LO, m, :], in0=slot[:, 0, m, :], scalar=bias[:, m:m + 1],
                                           in1=fl(qks[:, HI, m, :]), op0=ALU.add, op1=ALU.subtract).then_inc(qk_lo, 1)

            def row_stats(b, raw):
                for t in range(T):
                    last = V.bn_stats(st[:, t, :], Xf[:, ds(b * (T * S) + t * S, S)])
                last.then_inc(raw, 1)

            def mean_variance(ready):
                for t in range(T):
                    last = V.bn_aggr(mv[:, t, :], st[:, t, :])
                last.then_inc(ready, 1)

            def softmax_max(b):
                for h in range(2):
                    dve.wait_ge(score_done, b * T + 2 * h + 2)
                    V.tensor_reduce(nmax[:, 2 * h:2 * h + 2], sc[:, 2 * h:2 * h + 2, :], AX.X, ALU.max,
                                    negate=True).then_inc(max_ready, 1)

            def softmax_norm(b):
                for h in range(2):
                    dve.wait_ge(exp_done, b * T + 2 * h + 2)
                    V.reciprocal(rinv[:, 2 * h:2 * h + 2], rsum[:, 2 * h:2 * h + 2]).then_inc(inv_ready, 1)
                    dve.wait_ge(inv_ready, 2 * b + h + 1)
                    for t in (2 * h, 2 * h + 1):
                        V.tensor_scalar(work[:, t, :], work[:, t, :], rinv[:, t:t + 1], None, ALU.mult).then_inc(attn_ready, 1)

            def turned_lo_half(b, h, dst, done, n):
                dve.wait_ge(turned_hi, 2 * b + h + 1)
                V.tensor_tensor(dst[:, LO, 2 * h:2 * h + 2, :], sc[:, 2 * h:2 * h + 2, :],
                                fl(dst[:, HI, 2 * h:2 * h + 2, :]), ALU.subtract).then_inc(done, n)

            def x1(b, t):
                dve.wait_ge(mix_done, b * T + t + 1)
                dve.wait_ge(shifted, b * T + t + 1)
                row = Xf[:, ds(b * (T * S) + t * S, S)]
                V.scalar_tensor_tensor(out=row, in0=slot[:, 1, t % 2, :], scalar=s1[:, ds(b * T + t, 1)],
                                       in1=row, op0=ALU.mult, op1=ALU.add).then_inc(mix_free, 1)

            def weights_check(b, m):
                dve.wait_ge(w_hi, b * W3 + m + 1)
                V.scalar_tensor_tensor(out=wraw[:, m, :], in0=wraw[:, m, :], scalar=1.0,
                                       in1=fl(Whi[:, m, ds(b * WCH, WCH)]), op0=ALU.mult, op1=ALU.not_equal,
                                       accum_out=odd[:, ds(b * W3 + m, 1)]).then_inc(w_checked, 1)

            def norm(b):
                dve.wait_ge(rstd2_ready, b + 1)
                for t in range(T):
                    V.tensor_scalar(xraw[:, t, :], Xf[:, ds(b * (T * S) + t * S, S)], mv[:, t, 0:1], rs[:, t:t + 1],
                                    ALU.subtract, ALU.mult).then_inc(normed, 1)

            dve.wait_ge(wqk_hi, 1)
            V.tensor_tensor(wqs[:, LO, :, :, :].rearrange("p m c d -> p (m c d)"), wqraw,
                            fl(wqs[:, HI, :, :, :].rearrange("p m c d -> p (m c d)")), ALU.subtract).then_inc(wqk_lo, 1)
            context_lo(0)
            project_lo(0)
            softmax_max(0)
            dve.wait_ge(x_in, DMA)
            row_stats(0, stats_raw)
            dve.wait_ge(stats_raw, 1)
            mean_variance(stats_ready)
            softmax_norm(0)
            dve.wait_ge(const_in, 2 * DMA)
            dve.wait_ge(tanh_ready, 1)
            V.tensor_scalar(dsb[:, :], dsb[:, :], tg[:, 1:2], None, ALU.mult).then_inc(dsb_ready, 1)
            with dve.Fori(0, B - 1) as b:
                context_lo(b + 1)
                for h in range(2):
                    turned_lo_half(b, h, mixT, turned_lo, 1)
                project_lo(b + 1)
                dve.wait_ge(x_in, (b + 2) * DMA)
                dve.wait_ge(scale_ready, b + 1)
                row_stats(b + 1, stats_raw)
                dve.wait_ge(stats_raw, b + 2)
                x1(b, 0)
                mean_variance(stats_ready)
                softmax_max(b + 1)
                x1(b, 1)
                softmax_norm(b + 1)
                x1(b, 2)
                weights_check(b, GATE)
                weights_check(b, UP)
                x1(b, 3)
                weights_check(b, DOWN)
            for h in range(2):
                turned_lo_half(B - 1, h, mixT, turned_lo, 1)
            dve.wait_ge(scale_ready, B)
            row_stats(0, stats2_raw)
            dve.wait_ge(stats2_raw, 1)
            mean_variance(stats2_ready)
            dve.wait_ge(xt_lo, B * T)
            norm(0)
            x1(B - 1, 0)
            x1(B - 1, 1)
            for h in range(2):
                turned_lo_half(B, h, actT[:, 1], out_free, 2)
            x1(B - 1, 2)
            for m in range(W3):
                weights_check(B - 1, m)
            x1(B - 1, 3)
            dve.wait_ge(w_checked, B * W3)
            V.reduce_sum(oddp[:, :], odd[:, :], AX.X).then_inc(odd_summed, 1)
            dve.wait_ge(odd_total, 1)
            V.tensor_scalar(flag[:, :], slot[0:1, 0, 0, 0:1], 0.0, None, ALU.is_gt).then_inc(flag_ready, 1)

            def phase_b(general):
                def unit(b, i, e, s):
                    if not (isinstance(b, int) and b == 0 and i == 0):
                        dve.wait_ge(hid_lo, b * NU + i)
                    dve.wait_ge(silu_done, b * NU + i + 1)
                    V.scalar_tensor_tensor(out=hid[:, s, :], in0=slot[:, s, UP, :], scalar=usc[:, UP, i % NU:i % NU + 1],
                                           in1=craw[:, s, :], op0=ALU.mult, op1=ALU.mult).then_inc(slot_free, 1)
                    dve.wait_ge(hid_hi, b * NU + i + 1)
                    V.tensor_tensor(mixT[:, LO, (i % NU) % T, :], hid[:, s, :], fl(mixT[:, HI, (i % NU) % T, :]),
                                    ALU.subtract).then_inc(hid_lo, 1)

                def batch(b, last):
                    turns = 0
                    for kind, what, e, s in events(b, last):
                        if kind == "unit":
                            if what == STATS_AFTER + 1 and not last:
                                dve.wait_ge(stats2_raw, b + 2)
                            unit(b, what, e, s)
                            if what == STATS_AFTER and not last:
                                row_stats(b + 1, stats2_raw)
                            if what == STATS_AFTER + 1 and not last:
                                mean_variance(stats2_ready)
                            if what == NORM_AFTER and not last:
                                norm(b + 1)
                        else:
                            turns += 1
                            dve.wait_ge(turned_hi, 2 * (B + 1) + b * NTURN + turns)
                            at, n = (b % 2) * (2 * T * S), len(what) * S
                            V.tensor_tensor(actf[:, ds(at + (LO * T + what[0]) * S, n)],
                                            slot[:, s, 0:len(what), :].rearrange("p k s -> p (k s)"),
                                            fl(actf[:, ds(at + (HI * T + what[0]) * S, n)]), ALU.subtract).then_inc(slot_free, 1)
                    dve.wait_ge(down_done, (b + 1) * NU)
                    for t in range(T):
                        if t >= 2:
                            dve.wait_ge(y_ready, b * T + t - 1)
                        elif last and t == 0:
                            dve.wait_ge(y_ready, b * T)
                        V.tensor_tensor(scaled[:, t % 2, :], sc[:, t, :], dsb[:, :], ALU.mult).then_inc(out_free, 1)

                unit(0, 0, 0, 0)
                dve.wait_ge(dsb_ready, 1)
                with dve.Fori(0, B - 1) as b:
                    batch(b, False)
                batch(B - 1, True)

            by_weights(dve, phase_b)

        @block.gpsimd
        def _(pool):
            G = nc.gpsimd
            small = [0]

            G.memset(half[:, :], -0.5)
            G.memset(zero[:, :], 0.0).then_inc(const_set, 1)
            G.memset(epst[:, :], EPS).then_inc(const_set, 1)
            G.memset(ones[:, :], 1.0).then_inc(ident_ready, 1)
            G.memset(start[:, 0:1], 0.0).then_inc(mix_free, 2)
            G.memset(start[:, 1:2], 0.0).then_inc(slot_free, 2)
            G.memset(ident[:, :], 1.0).then_inc(ident_set, 1)
            pool.wait_ge(ident_set, 1)
            G.affine_select(out=ident[:, :], in_=ident[:, :], compare_op=ALU.is_equal, fill=0.0, base=0,
                            pattern=[[-1, P]], channel_multiplier=1).then_inc(ident_ready, 1)

            def split_x(b, t):
                cols = slice(t * P, (t + 1) * P)
                G.tensor_tensor(actT[:, 0, HI, :, cols], xraw[:, :, cols],
                                zero[:, 0:1].unsqueeze(1).to_broadcast([P, T, P]), ALU.add).then_inc(xt_hi, 1)
                pool.wait_ge(xt_hi, b * T + t + 1)
                G.tensor_tensor(actT[:, 0, LO, :, cols], xraw[:, :, cols], fl(actT[:, 0, HI, :, cols]),
                                ALU.subtract).then_inc(xt_lo, 1)

            def rstd(step):
                G.tensor_tensor(ve[:, :], mv[:, :, 1], epst[:, :], ALU.add).then_inc(pool_step, 1)
                pool.wait_ge(pool_step, step)
                return G.tensor_tensor(rs[:, :], ve[:, :], half[:, :], ALU.pow)

            def scale_x(b):
                pool.wait_ge(stats_ready, b + 1)
                rstd(2 * b + 1).then_inc(pool_step, 1)
                G.tensor_scalar(ms[:, :], mv[:, :, 0], -1.0, None, ALU.mult)
                pool.wait_ge(pool_step, 2 * b + 2)
                G.tensor_tensor(s1[:, ds(b * T, T)], rs[:, :], tg[:, 0:1].to_broadcast([P, T]), ALU.mult).then_inc(xt_scaled, 1)
                pool.wait_ge(xt_scaled, b + 1)
                G.tensor_tensor(nb[:, ds(b * T, T)], ms[:, :], s1[:, ds(b * T, T)], ALU.mult).then_inc(scale_ready, 1)

            pool.wait_ge(const_set, 2)
            pool.wait_ge(xt_in, DMA)
            split_x(0, 0)
            split_x(0, 1)
            pool.wait_ge(tanh_ready, 1)
            scale_x(0)
            split_x(0, 2)
            split_x(0, 3)
            with pool.Fori(0, B - 1) as b:
                pool.wait_ge(xt_in, (b + 2) * DMA)
                for t in range(T):
                    pool.wait_ge(mix_done, b * T + t + 1)
                    split_x(b + 1, t)
                    if t == 0:
                        scale_x(b + 1)

            def rstd2(b):
                pool.wait_ge(stats2_ready, b + 1)
                rstd(2 * B + b + 1).then_inc(rstd2_ready, 1)

            rstd2(0)

            def phase_b(general):
                def low_weights(b, i):
                    u, c = b * NU + i, (i % NU) * P
                    pool.wait_ge(raw_in, (u + 1) * W3 * DMA)
                    if not isinstance(b, int) or u > 0:
                        pool.wait_ge(silu_done, u)
                    for m in (GATE, UP):
                        last = G.tensor_tensor(wlo_gu[:, m * T * P:(m + 1) * T * P].rearrange("p (k c) -> p k c", c=P),
                                               wraw[:, m, 0:T * P].rearrange("p (k c) -> p k c", c=P),
                                               fl(Whi[:, m, :]).rearrange("p (k f) -> p k f", f=F)[:, :, c:c + P], ALU.subtract)
                    last.then_inc(wlo_gu_ready, 1)
                    if not isinstance(b, int) or u > 0:
                        pool.wait_ge(down_done, u)
                    G.tensor_tensor(wlo_dn[:, 0:S], wraw[:, DOWN, 0:S], fl(Whi[:, DOWN, (i % NU) * S:(i % NU + 1) * S]),
                                    ALU.subtract).then_inc(wlo_dn_ready, 1)

                def batch(b, last):
                    for kind, what, e, s in events(b, last):
                        if kind == "unit":
                            if general:
                                low_weights(b, what)
                            if what == STATS_AFTER and not last:
                                rstd2(b + 1)
                    for t in range(T):
                        pool.wait_ge(out_free, (b + 1) * T + t + 1)
                        row = Xf[:, ds(b * (T * S) + t * S, S)]
                        G.tensor_tensor(row, row, scaled[:, t % 2, :], ALU.add).then_inc(y_ready, 1)

                if general:
                    low_weights(0, 0)
                with pool.Fori(0, B - 1) as b:
                    batch(b, False)
                batch(B - 1, True)

            by_weights(pool, phase_b)


def kernel(**inputs):
    import numpy as np
    import concourse.bacc as bacc
    from concourse.bass_utils import run_bass_kernel_spmd

    a = {k: np.asarray(v) for k, v in inputs.items()}

    def rows(w, tiles):
        return w.reshape(tiles, P, -1).transpose(1, 0, 2).reshape(P, -1)

    arrays = {
        "x": a["x"],
        "xT": a["x"].transpose(0, 2, 1),
        "ctxT": a["ctx_1024"].transpose(0, 2, 1),
        "wqk": np.stack([a["L0_xattn_Wq"].T, a["L0_xattn_Wk"].T]),
        "bqk": np.stack([a["L0_xattn_bq"], a["L0_xattn_bk"]], axis=1),
        "gates": np.concatenate([a["g_xattn"], a["g_ffn"]]),
        "w3": np.stack([rows(a["L0_ffn_gate_w"].T, T), rows(a["L0_ffn_up_w"].T, T), rows(a["L0_ffn_down_w"].T, NU)]),
        "scales": np.concatenate([a["L0_ffn_gate_s"].reshape(NU, P).T, a["L0_ffn_up_s"].reshape(NU, P).T], axis=1),
        "down_s": a["L0_ffn_down_s"],
    }
    arrays = {k: np.ascontiguousarray(v) for k, v in arrays.items()}
    nc = bacc.Bacc("TRN2", target_bir_lowering=False, num_devices=1)
    args = [nc.dram_tensor(k, v.shape, mybir.dt.from_np(v.dtype), kind="ExternalInput").ap() for k, v in arrays.items()]
    out = nc.dram_tensor("out", (B, S, S), mybir.dt.float32, kind="ExternalOutput").ap()
    flamingo_kernel(nc, *args, out)
    return run_bass_kernel_spmd(nc, [arrays], core_ids=[0]).results[0]["out"]
```

```python
import concourse.bass as bass
from concourse import mybir
from concourse.alu_op_type import AluOpType as ALU
from contextlib import ExitStack

P = 128
B, S, C, D, F = 4, 512, 256, 128, 1408
T = S // P
CT = C // P
NU = F // P
NP = 3 * T
EPS = 1e-5
HI, LO = 0, 1
Q, K = 0, 1
GATE, UP, DOWN = 0, 1, 2
W3 = 3
WARM_UP = 18
DMA = 16

EVENTS = [("unit", 1), ("unit", 2), ("unit", 3), ("unit", 4), ("unit", 5), ("turn", (0, 1)),
          ("unit", 6), ("turn", (2,)), ("unit", 7), ("turn", (3,)), ("unit", 8), ("unit", 9), ("unit", 10),
          ("unit", NU)]
LAST_EVENTS = [e for e in EVENTS if e[0] == "unit" and e[1] < NU]
NE = len(EVENTS)
NTURN = sum(e[0] == "turn" for e in EVENTS)
STATS_AFTER, NORM_AFTER = 2, 4


def flamingo_kernel(nc, x, xT, ctxT, wqk, bqk, gates, w3, scales, down_s, out):
    f32, f32r, i32 = mybir.dt.float32, mybir.dt.float32r, mybir.dt.int32
    ACT = mybir.ActivationFunctionType
    AX = mybir.AxisListType
    ds = bass.ds

    x_rows = x.rearrange("b (t p) n -> b p t n", p=P)
    out_rows = out.rearrange("b (t p) n -> b p t n", p=P)
    xT_rows = xT.rearrange("b (k p) l -> b p k l", p=P)
    ctxT_rows = ctxT.rearrange("b (c p) s -> b p c s", p=P)

    with ExitStack() as stack:
        def sb(name, shape, dt=f32):
            return stack.enter_context(nc.sbuf_tensor(name, shape, dt))

        def sem(name):
            return stack.enter_context(nc.semaphore(name))

        X = sb("X", [P, B * T, S])
        Whi = sb("Whi", [P, W3, T * F], f32r)
        wraw = sb("wraw", [P, W3, F])
        actT = sb("actT", [P, 2, 2, T, S], f32r)
        mixT = sb("mixT", [P, 2, T, S], f32r)
        work = sb("work", [P, T, S])
        xraw = sb("xraw", [P, T, S])
        craw = sb("craw", [P, CT, S])
        csp = sb("csp", [P, 2, CT, S], f32r)
        qks = sb("qks", [P, 2, 2, S], f32r)
        wqs = sb("wqs", [P, 2, 2, CT, D], f32r)
        dsb = sb("dsb", [P, S])
        ident = sb("ident", [P, P])
        ones = sb("ones", [P, 1])
        half = sb("half", [P, T])
        zero = sb("zero", [P, 1])
        start = sb("start", [P, 2])
        epst = sb("epst", [P, T])
        bias = sb("bias", [P, 2])
        g2 = sb("g2", [P, 2])
        tg = sb("tg", [P, 2])
        usc = sb("usc", [P, 2, NU])
        st = sb("st", [P, T, 6])
        mv = sb("mv", [P, T, 2])
        ve = sb("ve", [P, T])
        rs = sb("rs", [P, T])
        ms = sb("ms", [P, T])
        s1 = sb("s1", [P, B * T])
        nb = sb("nb", [P, B * T])
        nmax = sb("nmax", [P, T])
        rsum = sb("rsum", [P, T])
        rinv = sb("rinv", [P, T])
        odd = sb("odd", [P, NP])
        oddp = sb("oddp", [P, 1])
        flag = sb("flag", [1, 1], i32)
        wqraw = work[:, 0, :]
        hid = work[:, 2:4, :]
        scaled = [work[:, 0, :], work[:, 1, :], wraw[:, 0, F - S:F], wraw[:, 1, F - S:F]]
        Whi_flat = Whi[:, :, :].rearrange("p m f -> p (m f)")
        wlo_gu = csp[:, :, :, :].rearrange("p a c s -> p (a c s)")
        wlo_dn = qks[:, :, :, :].rearrange("p a c s -> p (a c s)")
        actf = actT[:, :, :, :, :].rearrange("p e a k s -> p (e a k s)")
        Xf = X[:, :, :].rearrange("p t n -> p (t n)")

        def fl(ap):
            return ap.bitcast(f32)

        sc = stack.enter_context(nc.psum_tensor("sc", [P, T, S], f32))
        slot = stack.enter_context(nc.psum_tensor("slot", [P, 2, 2, S], f32))

        ctx_in, wqk_in, small_in, xt_in, x_in, const_in = (sem(n) for n in (
            "ctx_in", "wqk_in", "small_in", "xt_in", "x_in", "const_in"))
        w_in = [sem(f"w_in{n}") for n in range(W3)]
        ident_set, ident_ready = sem("ident_set"), sem("ident_ready")
        wqk_hi, wqk_lo, ctx_hi, ctx_lo = sem("wqk_hi"), sem("wqk_lo"), sem("ctx_hi"), sem("ctx_lo")
        proj_done, qk_hi, qk_lo = sem("proj_done"), sem("qk_hi"), sem("qk_lo")
        score_done, max_ready, exp_done, inv_ready, attn_ready = (sem(n) for n in (
            "score_done", "max_ready", "exp_done", "inv_ready", "attn_ready"))
        turned, turned_hi, turned_lo = sem("turned"), sem("turned_hi"), sem("turned_lo")
        xt_hi, xt_lo = sem("xt_hi"), sem("xt_lo")
        stats_raw, stats_ready, pool_step, scale_ready, tanh_ready = (sem(n) for n in (
            "stats_raw", "stats_ready", "pool_step", "scale_ready", "tanh_ready"))
        xt_scaled, const_set = sem("xt_scaled"), sem("const_set")
        x1_added, mix_scaled, shifted, mix_done, mix_free = sem("x1_added"), sem("mix_scaled"), sem("shifted"), sem("mix_done"), sem("mix_free")
        w_hi, w_checked, odd_summed, odd_total, flag_ready, dsb_ready = (sem(n) for n in (
            "w_hi", "w_checked", "odd_summed", "odd_total", "flag_ready", "dsb_ready"))
        stats2_raw, stats2_ready, rstd2_ready, normed = (sem(n) for n in (
            "stats2_raw", "stats2_ready", "rstd2_ready", "normed"))
        slot_ready, slot_free, silu_done, hid_hi, hid_lo, down_done = (sem(n) for n in (
            "slot_ready", "slot_free", "silu_done", "hid_hi", "hid_lo", "down_done"))
        out_free, bank_done, y_ready, y_last, y_out = (sem(n) for n in ("out_free", "bank_done", "y_ready", "y_last", "y_out"))
        raw_in, wlo_gu_ready, wlo_dn_ready = sem("raw_in"), sem("wlo_gu_ready"), sem("wlo_dn_ready")

        block = stack.enter_context(nc.Block())

        def by_weights(eng, program):
            eng.wait_ge(flag_ready, 1)
            some = eng.value_load(flag[0:1, 0:1], min_val=0, max_val=1)
            with eng.If(some > 0):
                program(True)
            with eng.Else():
                program(False)

        def events(b, last):
            for j, (kind, what) in enumerate(LAST_EVENTS if last else EVENTS):
                yield kind, what, b * NE + 1 + j, (1 + j) % 2

        @block.sync
        def _(sp):
            def load_piece(j, n):
                sp.dma_start(wraw[:, n, :], w3[ds(W3 * j + n, 1)].rearrange("o p f -> (o p) f")).then_inc(w_in[n], DMA)

            sp.dma_start(wqraw.rearrange("p (m c d) -> p m c d", m=2, c=CT),
                         wqk.rearrange("m (c p) d -> p m c d", p=P)).then_inc(wqk_in, DMA)
            sp.dma_start(craw[:, :, :], ctxT_rows[0]).then_inc(ctx_in, DMA)
            sp.dma_start(bias[:, :], bqk).then_inc(small_in, DMA)
            sp.dma_start(g2[:, :], gates.partition_broadcast(P)).then_inc(small_in, DMA)
            def load_context(b):
                sp.wait_ge(ctx_lo, b)
                sp.dma_start(craw[:, :, :], ctxT_rows[ds(b, 1)].rearrange("o p c s -> (o p) c s")).then_inc(ctx_in, DMA)

            def load_x(b):
                sp.wait_ge(x_in, b * DMA)
                sp.dma_start(Xf[:, ds(b * (T * S), T * S)].rearrange("p (t n) -> p t n", n=S),
                             x_rows[ds(b, 1)].rearrange("o p t n -> (o p) t n")).then_inc(x_in, DMA)

            def loads(b, more):
                if more:
                    load_context(b + 2)
                sp.wait_ge(xt_lo, (b + 1) * T)
                sp.dma_start(xraw[:, :, :], xT_rows[ds(b + 1, 1)].rearrange("o p k l -> (o p) k l")).then_inc(xt_in, DMA)
                for n in range(W3):
                    sp.wait_ge(w_checked, b * W3 + n + 1)
                    load_piece(b + 1, n)
                    if n == 0 and more:
                        load_x(b + 2)

            sp.dma_start(xraw[:, :, :], xT_rows[0]).then_inc(xt_in, DMA)
            load_context(1)
            sp.dma_start(X[:, 0:T, :], x_rows[0]).then_inc(x_in, DMA)
            load_piece(0, 0)
            sp.dma_start(usc[:, :, :].rearrange("p a u -> p (a u)"), scales).then_inc(const_in, DMA)
            sp.dma_start(dsb[:, :], down_s.partition_broadcast(P)).then_inc(const_in, DMA)
            load_piece(0, 1)
            load_piece(0, 2)
            load_x(1)
            with sp.Fori(0, B - 2) as b:
                loads(b, True)
            loads(B - 2, False)

            def phase_b(general):
                def raw_weights(b, i):
                    u, c = b * NU + i, (i % NU) * P
                    if not isinstance(b, int) or u > 0:
                        sp.wait_ge(wlo_dn_ready, u)
                    for m in (GATE, UP):
                        sp.dma_start(wraw[:, m, 0:T * P].rearrange("p (k c) -> p k c", c=P),
                                     w3[m * T:(m + 1) * T, :, c:c + P].rearrange("k p c -> p k c")).then_inc(raw_in, DMA)
                    for q in range(T):
                        at = (i % NU) * S + q * P
                        sp.dma_start(wraw[:, DOWN, q * P:(q + 1) * P],
                                     w3[DOWN * T + at // F, :, at % F:at % F + P]).then_inc(raw_in, DMA)

                def batch(b, last):
                    if general:
                        for kind, i, _, _ in events(b, last):
                            if kind == "unit":
                                raw_weights(b, i)
                    if not last:
                        sp.wait_ge(y_ready, (b + 1) * T)
                        sp.dma_start(out_rows[ds(b, 1)].rearrange("o p t n -> (o p) t n"),
                                     Xf[:, ds(b * (T * S), T * S)].rearrange("p (t n) -> p t n", n=S)).then_inc(y_out, DMA)
                    else:
                        for t, done, count in ((0, y_ready, b * T + 1), (1, y_last, 1), (2, y_ready, b * T + 2), (3, y_last, 2)):
                            sp.wait_ge(done, count)
                            sp.dma_start(out_rows[b][:, t, :], X[:, b * T + t, :]).then_inc(y_out, DMA)

                if general:
                    raw_weights(0, 0)
                with sp.Fori(0, B - 1) as b:
                    batch(b, False)
                batch(B - 1, True)
                sp.wait_ge(y_out, (B - 1 + T) * DMA)

            by_weights(sp, phase_b)

        @block.tensor
        def _(pe):
            MM = nc.tensor.matmul

            def project(b):
                pe.wait_ge(ctx_hi, b + 1)
                for m in (Q, K):
                    steps = [(wp, cp, c) for wp, cp in ((HI, HI), (LO, HI), (HI, LO)) for c in range(CT)]
                    for n, (wp, cp, c) in enumerate(steps):
                        if m == Q and n == 2 * CT:
                            pe.wait_ge(ctx_lo, b + 1)
                        last = MM(slot[:, 0, m, :], wqs[:, wp, m, c, :], csp[:, cp, c, :],
                                  start=(n == 0), stop=(n == len(steps) - 1))
                    last.then_inc(proj_done, 1)

            def scores(b):
                pe.wait_ge(qk_lo, 2 * b + 2)
                for t in range(T):
                    for n, (qp, kp) in enumerate(((HI, HI), (LO, HI), (HI, LO))):
                        last = MM(sc[:, t, :], qks[:, qp, Q, t * P:(t + 1) * P], qks[:, kp, K, :],
                                  start=(n == 0), stop=(n == 2))
                    last.then_inc(score_done, 1)

            def turn(bank, src, k):
                for t in range(T):
                    last = nc.tensor.transpose(bank[:, t * P:(t + 1) * P], src[:, t, k * P:(k + 1) * P], ident[:, :])
                return last

            def turn_attention(b):
                pe.wait_ge(attn_ready, (b + 1) * T)
                for k in range(T):
                    last = turn(sc[:, k, :], work, k)
                    if k % 2:
                        last.then_inc(turned, 1)

            def mix(b, t):
                pe.wait_ge(mix_free, b * T + t + 1)
                pe.wait_ge(xt_lo, b * T + t + 1)
                steps = ([(k, xp, HI) for k in range(T) for xp in (HI, LO)] + [(k, HI, LO) for k in range(T)])
                for n, (k, xp, ap) in enumerate(steps):
                    if t == 0 and k % 2 == 0 and xp == HI:
                        pe.wait_ge((turned_hi, turned_lo)[ap], 2 * b + k // 2 + 1)
                    last = MM(slot[:, 1, t % 2, :], actT[:, 0, xp, k, t * P:(t + 1) * P], mixT[:, ap, k, :],
                              start=(n == 0), stop=(n == len(steps) - 1))
                last.then_inc(mix_done, 1)

            pe.wait_ge(ident_ready, 2)
            for n in range(WARM_UP):
                MM(sc[:, 0, 0:P], ident[:, :], ident[:, :], start=True, stop=True)
            pe.wait_ge(wqk_lo, 1)
            project(0)
            scores(0)
            with pe.Fori(0, B - 1) as b:
                turn_attention(b)
                project(b + 1)
                mix(b, 0)
                scores(b + 1)
                for t in range(1, T):
                    mix(b, t)
            turn_attention(B - 1)
            mix(B - 1, 0)
            mix(B - 1, 1)
            mix(B - 1, 2)
            mix(B - 1, 3)
            pe.wait_ge(normed, T)
            for k in range(T):
                last = turn(sc[:, k, :], xraw, k)
                if k % 2:
                    last.then_inc(turned, 1)
            pe.wait_ge(odd_summed, 1)
            MM(slot[0:1, 0, 0, 0:1], oddp[:, 0:1], ones[:, 0:1], start=True, stop=True).then_inc(odd_total, 1)

            def phase_b(general):
                parts = ((HI, HI), (HI, LO), (LO, HI))[:3 if general else 2]

                def gate_up(b, i, s, first=False):
                    c, buf = (i % NU) * P, (b + 1 + i // NU) % 2
                    if general:
                        pe.wait_ge(wlo_gu_ready, b * NU + i + 1)
                    steps = [(m, k, n) for m in (GATE, UP) for k in range(T) for n in range(len(parts))]
                    if first:
                        steps.sort(key=lambda step: (step[2], step[1]))
                    for m, k, n in steps:
                        wp, ap = parts[n]
                        if first and m == GATE and k % 2 == 0 and n < 2:
                            if ap == HI:
                                pe.wait_ge(turned_hi, 2 * B + k // 2 + 1)
                            else:
                                pe.wait_ge(out_free, k + 2)
                        w = Whi[:, m, k * F + c:k * F + c + P] if wp == HI else wlo_gu[:, (m * T + k) * P:(m * T + k + 1) * P]
                        last = MM(slot[:, s, m, :], w, actf[:, ds(buf * (2 * T * S) + (ap * T + k) * S, S)],
                                  start=(k == 0 and n == 0), stop=(k == T - 1 and n == len(parts) - 1))
                    last.then_inc(slot_ready, 1)

                def down(b, i, high_first):
                    by_tile = [(t, n) for t in range(T) for n in range(len(parts))]
                    pe.wait_ge(hid_hi if high_first else hid_lo, b * NU + i + 1)
                    if general:
                        pe.wait_ge(wlo_dn_ready, b * NU + i + 1)
                    for step, (t, n) in enumerate(sorted(by_tile, key=lambda tn: tn[1] > 0) if high_first else by_tile):
                        if i == 0 and n == 0:
                            pe.wait_ge(out_free, b * T + t + 1)
                        if high_first and step == T:
                            pe.wait_ge(hid_lo, b * NU + i + 1)
                        wp, hp = parts[n]
                        w = Whi[:, DOWN, i * S:(i + 1) * S] if wp == HI else wlo_dn[:, 0:S]
                        last = MM(sc[:, t, :], mixT[:, hp, i % T, t * P:(t + 1) * P], w,
                                  start=(i == 0 and n == 0), stop=(i == NU - 1 and n == len(parts) - 1))
                        if i == NU - 1 and n == len(parts) - 1:
                            last.then_inc(bank_done, 1)
                    if i < NU - 1:
                        last.then_inc(down_done, 1)

                def batch(b, last):
                    late = last and not general
                    for kind, what, e, s in events(b, last):
                        pe.wait_ge(slot_free, e + 1)
                        if kind == "unit":
                            gate_up(b, what, s)
                            if not (late and what == NU - 2):
                                for i in range(what - (2 if late and what == NU - 1 else 1), what):
                                    down(b, i, False)
                        else:
                            for n, k in enumerate(what):
                                if k == 0:
                                    pe.wait_ge(normed, (b + 2) * T)
                                turned_now = turn(slot[:, s, n, :], xraw, k)
                            turned_now.then_inc(slot_ready, 1)
                    if last:
                        down(b, NU - 1, True)

                gate_up(0, 0, 0, first=True)
                pe.wait_ge(mix_scaled, 2)
                with pe.Fori(0, B - 1) as b:
                    batch(b, False)
                batch(B - 1, True)

            by_weights(pe, phase_b)

        @block.scalar
        def _(act):
            A = nc.scalar.activation

            def context_hi(b):
                act.wait_ge(ctx_in, (b + 1) * DMA)
                if not isinstance(b, int) or b > 0:
                    act.wait_ge(proj_done, 2 * b)
                A(csp[:, HI, :, :], craw[:, :, :], ACT.Copy).then_inc(ctx_hi, 1)

            def project_hi(b):
                for m in (Q, K):
                    act.wait_ge(proj_done, 2 * b + m + 1)
                    A(qks[:, HI, m, :], slot[:, 0, m, :], ACT.Identity, bias=bias[:, m:m + 1]).then_inc(qk_hi, 1)

            def exp(b):
                for t in range(T):
                    act.wait_ge(max_ready, b * T + t + 1)
                    A(work[:, t, :], sc[:, t, :], ACT.Exp, bias=nmax[:, t:t + 1],
                      accum_out=rsum[:, t:t + 1]).then_inc(exp_done, 1)

            def softmax(b):
                exp(b)
                for t in range(T):
                    act.wait_ge(inv_ready, 2 * b + t // 2 + 1)
                    A(work[:, t, :], work[:, t, :], ACT.Copy, scale=rinv[:, t:t + 1]).then_inc(attn_ready, 1)

            def turned_hi_half(b, h, dst):
                act.wait_ge(turned, 2 * b + h + 1)
                A(dst[:, 2 * h:2 * h + 2, :], sc[:, 2 * h:2 * h + 2, :], ACT.Copy).then_inc(turned_hi, 1)

            def shift(b, tiles):
                act.wait_ge(scale_ready, b + 1)
                for t in tiles:
                    row = Xf[:, ds(b * (T * S) + t * S, S)]
                    A(row, row, ACT.Identity, bias=nb[:, ds(b * T + t, 1)]).then_inc(shifted, 1)

            def weights_hi(j, n):
                act.wait_ge(w_in[n], (j + 1) * DMA)
                A(Whi_flat[:, ds((j * W3 + n) * F, F)], wraw[:, n, :], ACT.Copy).then_inc(w_hi, 1)

            act.wait_ge(wqk_in, DMA)
            A(wqs[:, HI, :, :, :].rearrange("p m c d -> p (m c d)"), wqraw, ACT.Copy).then_inc(wqk_hi, 1)
            context_hi(0)
            act.wait_ge(small_in, 2 * DMA)
            A(tg[:, :], g2[:, :], ACT.Tanh).then_inc(tanh_ready, 1)
            project_hi(0)
            context_hi(1)
            exp(0)
            weights_hi(0, 0)

            def attend(b, more, more2):
                for h in range(2):
                    turned_hi_half(b, h, mixT[:, HI])
                if more:
                    project_hi(b + 1)
                shift(b, (0, 1))
                if more2:
                    context_hi(b + 2)
                weights_hi(b, 1)
                if more:
                    shift(b, (2, 3))
                    softmax(b + 1)
                weights_hi(b, 2)
                if more:
                    weights_hi(b + 1, 0)

            with act.Fori(0, B - 2) as b:
                attend(b, True, True)
            attend(B - 2, True, False)
            attend(B - 1, False, False)

            def scaled_mix(t):
                act.wait_ge(mix_done, (B - 1) * T + t + 1)
                A(work[:, t - 2, :], slot[:, 1, t % 2, :], ACT.Identity, bias=nb[:, (B - 1) * T + t:(B - 1) * T + t + 1],
                  scale=s1[:, (B - 1) * T + t:(B - 1) * T + t + 1]).then_inc(mix_scaled, 1)

            scaled_mix(2)
            scaled_mix(3)
            for h in range(2):
                turned_hi_half(B, h, actT[:, 1, HI])

            def phase_b(general):
                def unit(b, i, e, s):
                    act.wait_ge(slot_ready, e + 1)
                    A(craw[:, s, :], slot[:, s, GATE, :], ACT.Silu, scale=usc[:, GATE, i % NU:i % NU + 1]).then_inc(silu_done, 1)
                    act.wait_ge(slot_free, e + 3)
                    A(mixT[:, HI, (i % NU) % T, :], hid[:, s, :], ACT.Copy).then_inc(hid_hi, 1)

                def batch(b, last):
                    for kind, what, e, s in events(b, last):
                        if kind == "unit":
                            unit(b, what, e, s)
                        else:
                            act.wait_ge(slot_ready, e + 1)
                            A(actf[:, ds((b % 2) * (2 * T * S) + (HI * T + what[0]) * S, len(what) * S)],
                              slot[:, s, 0:len(what), :].rearrange("p k s -> p (k s)"), ACT.Copy).then_inc(turned_hi, 1)

                unit(0, 0, 0, 0)
                with act.Fori(0, B - 1) as b:
                    batch(b, False)
                batch(B - 1, True)

            by_weights(act, phase_b)

        @block.vector
        def _(dve):
            V = nc.vector

            def project_lo(b):
                for m in (Q, K):
                    dve.wait_ge(qk_hi, 2 * b + m + 1)
                    V.scalar_tensor_tensor(out=qks[:, LO, m, :], in0=slot[:, 0, m, :], scalar=bias[:, m:m + 1],
                                           in1=fl(qks[:, HI, m, :]), op0=ALU.add, op1=ALU.subtract).then_inc(qk_lo, 1)

            def row_stats(b, tiles, raw):
                for t in tiles:
                    V.bn_stats(st[:, t, :], Xf[:, ds(b * (T * S) + t * S, S)]).then_inc(raw, 1)

            def mean_variance(ready):
                for t in range(T):
                    last = V.bn_aggr(mv[:, t, :], st[:, t, :])
                last.then_inc(ready, 1)

            def softmax_max(b, n):
                for t in range(0, T, n):
                    dve.wait_ge(score_done, b * T + t + n)
                    V.tensor_reduce(nmax[:, t:t + n], sc[:, t:t + n, :], AX.X, ALU.max, negate=True).then_inc(max_ready, n)

            def inverse_sums(b, h):
                dve.wait_ge(exp_done, b * T + 2 * h + 2)
                V.reciprocal(rinv[:, 2 * h:2 * h + 2], rsum[:, 2 * h:2 * h + 2]).then_inc(inv_ready, 1)

            def turned_lo_half(b, h, dst, done, n):
                dve.wait_ge(turned_hi, 2 * b + h + 1)
                V.tensor_tensor(dst[:, LO, 2 * h:2 * h + 2, :], sc[:, 2 * h:2 * h + 2, :],
                                fl(dst[:, HI, 2 * h:2 * h + 2, :]), ALU.subtract).then_inc(done, n)

            def x1(b, t):
                dve.wait_ge(mix_done, b * T + t + 1)
                dve.wait_ge(shifted, b * T + t + 1)
                row = Xf[:, ds(b * (T * S) + t * S, S)]
                V.scalar_tensor_tensor(out=row, in0=slot[:, 1, t % 2, :], scalar=s1[:, ds(b * T + t, 1)],
                                       in1=row, op0=ALU.mult, op1=ALU.add).then_inc(mix_free, 1)

            def weights_check(j, n):
                dve.wait_ge(w_hi, j * W3 + n + 1)
                V.scalar_tensor_tensor(out=wraw[:, n, :], in0=wraw[:, n, :], scalar=1.0,
                                       in1=fl(Whi_flat[:, ds((j * W3 + n) * F, F)]), op0=ALU.mult, op1=ALU.not_equal,
                                       accum_out=odd[:, ds(j * W3 + n, 1)]).then_inc(w_checked, 1)

            def norm(b):
                dve.wait_ge(rstd2_ready, b + 1)
                for t in range(T):
                    V.tensor_scalar(xraw[:, t, :], Xf[:, ds(b * (T * S) + t * S, S)], mv[:, t, 0:1], rs[:, t:t + 1],
                                    ALU.subtract, ALU.mult).then_inc(normed, 1)

            dve.wait_ge(wqk_hi, 1)
            V.tensor_tensor(wqs[:, LO, :, :, :].rearrange("p m c d -> p (m c d)"), wqraw,
                            fl(wqs[:, HI, :, :, :].rearrange("p m c d -> p (m c d)")), ALU.subtract).then_inc(wqk_lo, 1)
            dve.wait_ge(ctx_hi, 1)
            V.tensor_tensor(csp[:, LO, :, :], craw[:, :, :], fl(csp[:, HI, :, :]), ALU.subtract).then_inc(ctx_lo, 1)
            project_lo(0)
            softmax_max(0, 1)
            for h in range(2):
                inverse_sums(0, h)
                dve.wait_ge(inv_ready, h + 1)
                for t in (2 * h, 2 * h + 1):
                    V.tensor_scalar(work[:, t, :], work[:, t, :], rinv[:, t:t + 1], None, ALU.mult).then_inc(attn_ready, 1)
            dve.wait_ge(x_in, DMA)
            row_stats(0, range(T), stats_raw)
            dve.wait_ge(stats_raw, T)
            mean_variance(stats_ready)
            def attend(b):
                for h in range(2):
                    turned_lo_half(b, h, mixT, turned_lo, 1)
                project_lo(b + 1)
                weights_check(b, 0)
                dve.wait_ge(x_in, (b + 2) * DMA)
                dve.wait_ge(scale_ready, b + 1)
                row_stats(b + 1, (0,), stats_raw)
                x1(b, 0)
                row_stats(b + 1, (1,), stats_raw)
                softmax_max(b + 1, 2)
                row_stats(b + 1, (2,), stats_raw)
                inverse_sums(b + 1, 0)
                row_stats(b + 1, (3,), stats_raw)
                inverse_sums(b + 1, 1)
                dve.wait_ge(stats_raw, (b + 2) * T)
                x1(b, 1)
                mean_variance(stats_ready)
                weights_check(b, 1)
                x1(b, 2)
                weights_check(b, 2)
                x1(b, 3)

            with dve.Fori(0, B - 1) as b:
                attend(b)
            for h in range(2):
                turned_lo_half(B - 1, h, mixT, turned_lo, 1)
            weights_check(B - 1, 0)
            x1(B - 1, 0)
            dve.wait_ge(scale_ready, B)
            row_stats(0, range(T), stats2_raw)
            dve.wait_ge(stats2_raw, T)
            mean_variance(stats2_ready)
            x1(B - 1, 1)
            weights_check(B - 1, 1)
            dve.wait_ge(xt_lo, B * T)
            norm(0)
            weights_check(B - 1, 2)
            dve.wait_ge(w_checked, NP)
            V.reduce_sum(oddp[:, :], odd[:, :], AX.X).then_inc(odd_summed, 1)
            turned_lo_half(B, 0, actT[:, 1], out_free, 2)
            dve.wait_ge(odd_total, 1)
            V.tensor_scalar(flag[:, :], slot[0:1, 0, 0, 0:1], 0.0, None, ALU.is_gt).then_inc(flag_ready, 1)
            turned_lo_half(B, 1, actT[:, 1], out_free, 2)
            dve.wait_ge(const_in, 2 * DMA)
            V.tensor_scalar(dsb[:, :], dsb[:, :], tg[:, 1:2], None, ALU.mult).then_inc(dsb_ready, 1)

            def phase_b(general):
                def unit(b, i, e, s):
                    if not (isinstance(b, int) and b == 0 and i == 0):
                        dve.wait_ge(hid_lo, b * NU + i)
                    dve.wait_ge(silu_done, b * NU + i + 1)
                    V.scalar_tensor_tensor(out=hid[:, s, :], in0=slot[:, s, UP, :], scalar=usc[:, UP, i % NU:i % NU + 1],
                                           in1=craw[:, s, :], op0=ALU.mult, op1=ALU.mult).then_inc(slot_free, 1)
                    dve.wait_ge(hid_hi, b * NU + i + 1)
                    V.tensor_tensor(mixT[:, LO, (i % NU) % T, :], hid[:, s, :], fl(mixT[:, HI, (i % NU) % T, :]),
                                    ALU.subtract).then_inc(hid_lo, 1)

                def batch(b, last):
                    turns = 0
                    for kind, what, e, s in events(b, last):
                        if kind == "unit":
                            if what == STATS_AFTER + 1 and not last:
                                dve.wait_ge(stats2_raw, (b + 2) * T)
                            unit(b, what, e, s)
                            if what == STATS_AFTER and not last:
                                row_stats(b + 1, range(T), stats2_raw)
                            if what == STATS_AFTER + 1 and not last:
                                mean_variance(stats2_ready)
                            if what == NORM_AFTER and not last:
                                norm(b + 1)
                        else:
                            turns += 1
                            dve.wait_ge(turned_hi, 2 * (B + 1) + b * NTURN + turns)
                            at, n = (b % 2) * (2 * T * S), len(what) * S
                            V.tensor_tensor(actf[:, ds(at + (LO * T + what[0]) * S, n)],
                                            slot[:, s, 0:len(what), :].rearrange("p k s -> p (k s)"),
                                            fl(actf[:, ds(at + (HI * T + what[0]) * S, n)]), ALU.subtract).then_inc(slot_free, 1)
                    if not last:
                        for t in range(T):
                            dve.wait_ge(bank_done, b * T + t + 1)
                            V.tensor_tensor(scaled[t], sc[:, t, :], dsb[:, :], ALU.mult).then_inc(out_free, 1)
                    else:
                        dve.wait_ge(y_ready, b * T)
                        for n, t in enumerate((0, 2, 1, 3)):
                            dve.wait_ge(bank_done, b * T + t + 1)
                            V.tensor_tensor(scaled[t], sc[:, t, :], dsb[:, :], ALU.mult).then_inc(out_free, 1)
                            if t % 2:
                                dve.wait_ge(out_free, (b + 1) * T + n + 1)
                                V.tensor_tensor(X[:, b * T + t, :], X[:, b * T + t, :], scaled[t], ALU.add).then_inc(y_last, 1)

                unit(0, 0, 0, 0)
                dve.wait_ge(dsb_ready, 1)
                dve.wait_ge(x1_added, 2)
                with dve.Fori(0, B - 1) as b:
                    batch(b, False)
                batch(B - 1, True)

            by_weights(dve, phase_b)

        @block.gpsimd
        def _(pool):
            G = nc.gpsimd

            G.memset(half[:, :], -0.5)
            G.memset(zero[:, :], 0.0).then_inc(const_set, 1)
            G.memset(epst[:, :], EPS).then_inc(const_set, 1)
            G.memset(ones[:, :], 1.0).then_inc(ident_ready, 1)
            G.memset(start[:, 0:1], 0.0).then_inc(mix_free, 2)
            G.memset(start[:, 1:2], 0.0).then_inc(slot_free, 2)
            G.memset(ident[:, :], 1.0).then_inc(ident_set, 1)
            pool.wait_ge(ident_set, 1)
            G.affine_select(out=ident[:, :], in_=ident[:, :], compare_op=ALU.is_equal, fill=0.0, base=0,
                            pattern=[[-1, P]], channel_multiplier=1).then_inc(ident_ready, 1)

            def split_x(b, t):
                cols = slice(t * P, (t + 1) * P)
                G.tensor_tensor(actT[:, 0, HI, :, cols], xraw[:, :, cols],
                                zero[:, 0:1].unsqueeze(1).to_broadcast([P, T, P]), ALU.add).then_inc(xt_hi, 1)
                pool.wait_ge(xt_hi, b * T + t + 1)
                G.tensor_tensor(actT[:, 0, LO, :, cols], xraw[:, :, cols], fl(actT[:, 0, HI, :, cols]),
                                ALU.subtract).then_inc(xt_lo, 1)

            def context_lo(b):
                pool.wait_ge(ctx_hi, b + 1)
                G.tensor_tensor(csp[:, LO, :, :], craw[:, :, :], fl(csp[:, HI, :, :]), ALU.subtract).then_inc(ctx_lo, 1)

            def rstd(step):
                G.tensor_tensor(ve[:, :], mv[:, :, 1], epst[:, :], ALU.add).then_inc(pool_step, 1)
                pool.wait_ge(pool_step, step)
                return G.tensor_tensor(rs[:, :], ve[:, :], half[:, :], ALU.pow)

            def scale_x(b):
                pool.wait_ge(stats_ready, b + 1)
                rstd(2 * b + 1).then_inc(pool_step, 1)
                G.tensor_scalar(ms[:, :], mv[:, :, 0], -1.0, None, ALU.mult)
                pool.wait_ge(pool_step, 2 * b + 2)
                G.tensor_tensor(s1[:, ds(b * T, T)], rs[:, :], tg[:, 0:1].to_broadcast([P, T]), ALU.mult).then_inc(xt_scaled, 1)
                pool.wait_ge(xt_scaled, b + 1)
                G.tensor_tensor(nb[:, ds(b * T, T)], ms[:, :], s1[:, ds(b * T, T)], ALU.mult).then_inc(scale_ready, 1)

            pool.wait_ge(const_set, 2)
            pool.wait_ge(xt_in, DMA)
            split_x(0, 0)
            split_x(0, 1)
            context_lo(1)
            split_x(0, 2)
            split_x(0, 3)
            pool.wait_ge(tanh_ready, 1)
            scale_x(0)

            def attend(b, more2):
                pool.wait_ge(xt_in, (b + 2) * DMA)
                for t in range(T):
                    pool.wait_ge(mix_done, b * T + t + 1)
                    split_x(b + 1, t)
                    if t == 0:
                        if more2:
                            context_lo(b + 2)
                        scale_x(b + 1)

            with pool.Fori(0, B - 2) as b:
                attend(b, True)
            attend(B - 2, False)

            def rstd2(b):
                pool.wait_ge(stats2_ready, b + 1)
                rstd(2 * B + b + 1).then_inc(rstd2_ready, 1)

            rstd2(0)
            for t in (2, 3):
                pool.wait_ge(mix_scaled, t - 1)
                row = X[:, (B - 1) * T + t, :]
                G.tensor_tensor(row, row, work[:, t - 2, :], ALU.add).then_inc(x1_added, 1)

            def phase_b(general):
                def low_weights(b, i):
                    u, c = b * NU + i, (i % NU) * P
                    pool.wait_ge(raw_in, (u + 1) * (2 + T) * DMA)
                    if not isinstance(b, int) or u > 0:
                        pool.wait_ge(silu_done, u)
                    for m in (GATE, UP):
                        last = G.tensor_tensor(wlo_gu[:, m * T * P:(m + 1) * T * P].rearrange("p (k c) -> p k c", c=P),
                                               wraw[:, m, 0:T * P].rearrange("p (k c) -> p k c", c=P),
                                               fl(Whi[:, m, :]).rearrange("p (k f) -> p k f", f=F)[:, :, c:c + P], ALU.subtract)
                    last.then_inc(wlo_gu_ready, 1)
                    if i == NU:
                        pool.wait_ge(bank_done, (b + 1) * T)
                    elif i > 0:
                        pool.wait_ge(down_done, b * (NU - 1) + i)
                    G.tensor_tensor(wlo_dn[:, 0:S], wraw[:, DOWN, 0:S], fl(Whi[:, DOWN, (i % NU) * S:(i % NU + 1) * S]),
                                    ALU.subtract).then_inc(wlo_dn_ready, 1)

                def batch(b, last):
                    for kind, what, e, s in events(b, last):
                        if kind == "unit":
                            if general:
                                low_weights(b, what)
                            if what == STATS_AFTER + 2 and not last:
                                rstd2(b + 1)
                    for n, t in enumerate((0, 2) if last else range(T)):
                        pool.wait_ge(out_free, (b + 1) * T + n + 1)
                        row = Xf[:, ds(b * (T * S) + t * S, S)]
                        G.tensor_tensor(row, row, scaled[t], ALU.add).then_inc(y_ready, 1)

                if general:
                    low_weights(0, 0)
                with pool.Fori(0, B - 1) as b:
                    batch(b, False)
                batch(B - 1, True)

            by_weights(pool, phase_b)


def kernel(**inputs):
    import numpy as np
    import concourse.bacc as bacc
    from concourse.bass_utils import run_bass_kernel_spmd

    a = {k: np.asarray(v) for k, v in inputs.items()}

    def rows(w, tiles):
        return w.reshape(tiles, P, -1).transpose(1, 0, 2).reshape(P, -1)

    arrays = {
        "x": a["x"],
        "xT": a["x"].transpose(0, 2, 1),
        "ctxT": a["ctx_1024"].transpose(0, 2, 1),
        "wqk": np.stack([a["L0_xattn_Wq"].T, a["L0_xattn_Wk"].T]),
        "bqk": np.stack([a["L0_xattn_bq"], a["L0_xattn_bk"]], axis=1),
        "gates": np.concatenate([a["g_xattn"], a["g_ffn"]]),
        "w3": np.concatenate([rows(a[f"L0_ffn_{w}_w"].T, n).reshape(P, T, F).transpose(1, 0, 2)
                              for w, n in (("gate", T), ("up", T), ("down", NU))]),
        "scales": np.concatenate([a["L0_ffn_gate_s"].reshape(NU, P).T, a["L0_ffn_up_s"].reshape(NU, P).T], axis=1),
        "down_s": a["L0_ffn_down_s"],
    }
    arrays = {k: np.ascontiguousarray(v) for k, v in arrays.items()}
    nc = bacc.Bacc("TRN2", target_bir_lowering=False, num_devices=1)
    args = [nc.dram_tensor(k, v.shape, mybir.dt.from_np(v.dtype), kind="ExternalInput").ap() for k, v in arrays.items()]
    out = nc.dram_tensor("out", (B, S, S), mybir.dt.float32, kind="ExternalOutput").ap()
    flamingo_kernel(nc, *args, out)
    return run_bass_kernel_spmd(nc, [arrays], core_ids=[0]).results[0]["out"]
```

```python
import concourse.bass as bass
from concourse import mybir
from concourse.alu_op_type import AluOpType as ALU
from contextlib import ExitStack

P = 128
B, S, C, D, F = 4, 512, 256, 128, 1408
T = S // P
CT = C // P
NU = F // P
NP = 3 * T
EPS = 1e-5
HI, LO = 0, 1
Q, K = 0, 1
GATE, UP, DOWN = 0, 1, 2
W3 = 3
WARM_UP = 8
DMA = 16

EVENTS = [("unit", 1), ("unit", 2), ("unit", 3), ("unit", 4), ("unit", 5), ("turn", (0, 1)),
          ("unit", 6), ("turn", (2,)), ("unit", 7), ("turn", (3,)), ("unit", 8), ("unit", 9), ("unit", 10),
          ("unit", NU)]
LAST_EVENTS = [e for e in EVENTS if e[0] == "unit" and e[1] < NU]
NE = len(EVENTS)
NTURN = sum(e[0] == "turn" for e in EVENTS)
STATS_AFTER, NORM_AFTER = 2, 4


def flamingo_kernel(nc, x, xT, ctxT, wqk, bqk, gates, w3, scales, down_s, out):
    f32, f32r, i32 = mybir.dt.float32, mybir.dt.float32r, mybir.dt.int32
    ACT = mybir.ActivationFunctionType
    AX = mybir.AxisListType
    ds = bass.ds

    x_rows = x.rearrange("b (t p) n -> b p t n", p=P)
    out_rows = out.rearrange("b (t p) n -> b p t n", p=P)
    xT_rows = xT.rearrange("b (k p) l -> b p k l", p=P)
    ctxT_rows = ctxT.rearrange("b (c p) s -> b p c s", p=P)

    with ExitStack() as stack:
        def sb(name, shape, dt=f32):
            return stack.enter_context(nc.sbuf_tensor(name, shape, dt))

        def sem(name):
            return stack.enter_context(nc.semaphore(name))

        X = sb("X", [P, B * T, S])
        Whi = sb("Whi", [P, W3, T * F], f32r)
        wraw = sb("wraw", [P, W3, F])
        actT = sb("actT", [P, 2, 2, T, S], f32r)
        mixT = sb("mixT", [P, 2, T, S], f32r)
        work = sb("work", [P, T, S])
        xraw = sb("xraw", [P, T, S])
        craw = sb("craw", [P, CT, S])
        csp = sb("csp", [P, 2, CT, S], f32r)
        qks = sb("qks", [P, 2, 2, S], f32r)
        wqs = sb("wqs", [P, 2, 2, CT, D], f32r)
        dsb = sb("dsb", [P, S])
        ident = sb("ident", [P, P])
        ones = sb("ones", [P, 1])
        half = sb("half", [P, T])
        zero = sb("zero", [P, 1])
        start = sb("start", [P, 2])
        epst = sb("epst", [P, T])
        bias = sb("bias", [P, 2])
        g2 = sb("g2", [P, 2])
        tg = sb("tg", [P, 2])
        usc = sb("usc", [P, 2, NU])
        st = sb("st", [P, T, 6])
        mv = sb("mv", [P, T, 2])
        ve = sb("ve", [P, T])
        rs = sb("rs", [P, T])
        ms = sb("ms", [P, T])
        s1 = sb("s1", [P, B * T])
        nb = sb("nb", [P, B * T])
        nmax = sb("nmax", [P, T])
        rsum = sb("rsum", [P, T])
        rinv = sb("rinv", [P, T])
        odd = sb("odd", [P, NP])
        oddp = sb("oddp", [P, 1])
        flag = sb("flag", [1, 1], i32)
        wqraw = work[:, 0, :]
        hid = work[:, 2:4, :]
        scaled = [work[:, 0, :], work[:, 1, :], wraw[:, 0, F - S:F], wraw[:, 1, F - S:F]]
        Whi_flat = Whi[:, :, :].rearrange("p m f -> p (m f)")
        wlo_gu = csp[:, :, :, :].rearrange("p a c s -> p (a c s)")
        wlo_dn = qks[:, :, :, :].rearrange("p a c s -> p (a c s)")
        actf = actT[:, :, :, :, :].rearrange("p e a k s -> p (e a k s)")
        Xf = X[:, :, :].rearrange("p t n -> p (t n)")

        def fl(ap):
            return ap.bitcast(f32)

        sc = stack.enter_context(nc.psum_tensor("sc", [P, T, S], f32))
        slot = stack.enter_context(nc.psum_tensor("slot", [P, 2, 2, S], f32))

        ctx_in, wqk_in, small_in, xt_in, x_in, const_in = (sem(n) for n in (
            "ctx_in", "wqk_in", "small_in", "xt_in", "x_in", "const_in"))
        w_in = [sem(f"w_in{n}") for n in range(W3)]
        first_half_in, first_half_hi = sem("first_half_in"), sem("first_half_hi")
        ident_set, ident_ready = sem("ident_set"), sem("ident_ready")
        wqk_hi, wqk_lo, ctx_hi, ctx_lo = sem("wqk_hi"), sem("wqk_lo"), sem("ctx_hi"), sem("ctx_lo")
        proj_done, qk_hi, qk_lo = sem("proj_done"), sem("qk_hi"), sem("qk_lo")
        score_done, max_ready, exp_done, inv_ready, attn_ready = (sem(n) for n in (
            "score_done", "max_ready", "exp_done", "inv_ready", "attn_ready"))
        turned, turned_hi, turned_lo = sem("turned"), sem("turned_hi"), sem("turned_lo")
        xt_hi, xt_lo = sem("xt_hi"), sem("xt_lo")
        stats_raw, stats_ready, pool_step, scale_ready, tanh_ready = (sem(n) for n in (
            "stats_raw", "stats_ready", "pool_step", "scale_ready", "tanh_ready"))
        xt_scaled, const_set = sem("xt_scaled"), sem("const_set")
        shifted, mix_done, mix_free, mix_scaled, x1_added = (sem(n) for n in (
            "shifted", "mix_done", "mix_free", "mix_scaled", "x1_added"))
        w_hi, w_checked, odd_summed, odd_total, flag_ready, dsb_ready = (sem(n) for n in (
            "w_hi", "w_checked", "odd_summed", "odd_total", "flag_ready", "dsb_ready"))
        stats2_raw, stats2_ready, rstd2_ready, normed = (sem(n) for n in (
            "stats2_raw", "stats2_ready", "rstd2_ready", "normed"))
        slot_ready, slot_free, silu_done, hid_hi, hid_lo, down_done = (sem(n) for n in (
            "slot_ready", "slot_free", "silu_done", "hid_hi", "hid_lo", "down_done"))
        out_free, bank_done, y_ready, y_last, y_out = (sem(n) for n in (
            "out_free", "bank_done", "y_ready", "y_last", "y_out"))
        raw_in, wlo_gu_ready, wlo_dn_ready = sem("raw_in"), sem("wlo_gu_ready"), sem("wlo_dn_ready")

        block = stack.enter_context(nc.Block())

        def by_weights(eng, program):
            eng.wait_ge(flag_ready, 1)
            some = eng.value_load(flag[0:1, 0:1], min_val=0, max_val=1)
            with eng.If(some > 0):
                program(True)
            with eng.Else():
                program(False)

        def events(b, last):
            for j, (kind, what) in enumerate(LAST_EVENTS if last else EVENTS):
                yield kind, what, b * NE + 1 + j, (1 + j) % 2

        @block.sync
        def _(sp):
            def load_piece(j, n):
                sp.dma_start(wraw[:, n, :], w3[ds(W3 * j + n, 1)].rearrange("o p f -> (o p) f")).then_inc(w_in[n], DMA)

            sp.dma_start(wqraw.rearrange("p (m c d) -> p m c d", m=2, c=CT),
                         wqk.rearrange("m (c p) d -> p m c d", p=P)).then_inc(wqk_in, DMA)
            for c in range(CT):
                sp.dma_start(craw[:, c, :], ctxT_rows[0][:, c, :]).then_inc((first_half_in, ctx_in)[c], DMA)
            sp.dma_start(bias[:, :], bqk).then_inc(small_in, DMA)
            sp.dma_start(g2[:, :], gates.partition_broadcast(P)).then_inc(small_in, DMA)

            def load_context(b):
                sp.wait_ge(ctx_lo, b)
                sp.dma_start(craw[:, :, :], ctxT_rows[ds(b, 1)].rearrange("o p c s -> (o p) c s")).then_inc(ctx_in, DMA)

            def load_x(b):
                sp.wait_ge(x_in, b * DMA)
                sp.dma_start(Xf[:, ds(b * (T * S), T * S)].rearrange("p (t n) -> p t n", n=S),
                             x_rows[ds(b, 1)].rearrange("o p t n -> (o p) t n")).then_inc(x_in, DMA)

            def loads(b, more):
                if more:
                    load_context(b + 2)
                sp.wait_ge(xt_lo, (b + 1) * T)
                sp.dma_start(xraw[:, :, :], xT_rows[ds(b + 1, 1)].rearrange("o p k l -> (o p) k l")).then_inc(xt_in, DMA)
                for n in range(W3):
                    sp.wait_ge(w_checked, b * W3 + n + 1)
                    load_piece(b + 1, n)
                    if n == 0 and more:
                        load_x(b + 2)

            sp.dma_start(xraw[:, :, :], xT_rows[0]).then_inc(xt_in, DMA)
            load_context(1)
            sp.dma_start(X[:, 0:T, :], x_rows[0]).then_inc(x_in, DMA)
            load_piece(0, 0)
            sp.dma_start(usc[:, :, :].rearrange("p a u -> p (a u)"), scales).then_inc(const_in, DMA)
            sp.dma_start(dsb[:, :], down_s.partition_broadcast(P)).then_inc(const_in, DMA)
            load_piece(0, 1)
            load_piece(0, 2)
            load_x(1)
            with sp.Fori(0, B - 2) as b:
                loads(b, True)
            loads(B - 2, False)

            def phase_b(general):
                def raw_weights(b, i):
                    u, c = b * NU + i, (i % NU) * P
                    if not isinstance(b, int) or u > 0:
                        sp.wait_ge(wlo_dn_ready, u)
                    for m in (GATE, UP):
                        sp.dma_start(wraw[:, m, 0:T * P].rearrange("p (k c) -> p k c", c=P),
                                     w3[m * T:(m + 1) * T, :, c:c + P].rearrange("k p c -> p k c")).then_inc(raw_in, DMA)
                    for q in range(T):
                        at = (i % NU) * S + q * P
                        sp.dma_start(wraw[:, DOWN, q * P:(q + 1) * P],
                                     w3[DOWN * T + at // F, :, at % F:at % F + P]).then_inc(raw_in, DMA)

                def batch(b, last):
                    if general:
                        for kind, i, _, _ in events(b, last):
                            if kind == "unit":
                                raw_weights(b, i)
                    if not last:
                        sp.wait_ge(y_ready, (b + 1) * T)
                        sp.dma_start(out_rows[ds(b, 1)].rearrange("o p t n -> (o p) t n"),
                                     Xf[:, ds(b * (T * S), T * S)].rearrange("p (t n) -> p t n", n=S)).then_inc(y_out, DMA)
                    else:
                        for t, done, count in ((0, y_ready, b * T + 1), (1, y_last, 1), (2, y_ready, b * T + 2), (3, y_last, 2)):
                            sp.wait_ge(done, count)
                            sp.dma_start(out_rows[b][:, t, :], X[:, b * T + t, :]).then_inc(y_out, DMA)

                if general:
                    raw_weights(0, 0)
                with sp.Fori(0, B - 1) as b:
                    batch(b, False)
                batch(B - 1, True)
                sp.wait_ge(y_out, (B - 1 + T) * DMA)

            by_weights(sp, phase_b)

        @block.tensor
        def _(pe):
            MM = nc.tensor.matmul

            def project(b, first=False):
                pe.wait_ge(*((first_half_hi, 1) if first else (ctx_hi, b + 1)))
                for m in (Q, K):
                    steps = [(wp, cp, c) for wp, cp in ((HI, HI), (LO, HI), (HI, LO)) for c in range(CT)]
                    for n, (wp, cp, c) in enumerate(steps):
                        if first and m == Q and n == 1:
                            pe.wait_ge(ctx_hi, 1)
                        if m == Q and n == 2 * CT:
                            pe.wait_ge(ctx_lo, b + 1)
                        last = MM(slot[:, 0, m, :], wqs[:, wp, m, c, :], csp[:, cp, c, :],
                                  start=(n == 0), stop=(n == len(steps) - 1))
                    last.then_inc(proj_done, 1)

            def scores(b):
                pe.wait_ge(qk_hi, 2 * b + 2)
                for t in range(T):
                    MM(sc[:, t, :], qks[:, HI, Q, t * P:(t + 1) * P], qks[:, HI, K, :], start=True, stop=False)
                pe.wait_ge(qk_lo, 2 * b + 2)
                for t in range(T):
                    MM(sc[:, t, :], qks[:, LO, Q, t * P:(t + 1) * P], qks[:, HI, K, :], start=False, stop=False)
                    MM(sc[:, t, :], qks[:, HI, Q, t * P:(t + 1) * P], qks[:, LO, K, :],
                       start=False, stop=True).then_inc(score_done, 1)

            def turn(bank, src, k):
                for t in range(T):
                    last = nc.tensor.transpose(bank[:, t * P:(t + 1) * P], src[:, t, k * P:(k + 1) * P], ident[:, :])
                return last

            def turn_attention(b):
                pe.wait_ge(attn_ready, (b + 1) * T)
                for k in range(T):
                    last = turn(sc[:, k, :], work, k)
                    if k % 2:
                        last.then_inc(turned, 1)

            def mix(b, t):
                if not isinstance(b, int) or b < B - 1 or t < 2:
                    pe.wait_ge(mix_free, b * T + t + 1)
                else:
                    pe.wait_ge(mix_scaled, t - 1)
                pe.wait_ge(xt_lo, b * T + t + 1)
                steps = ([(k, xp, HI) for k in range(T) for xp in (HI, LO)] + [(k, HI, LO) for k in range(T)])
                for n, (k, xp, ap) in enumerate(steps):
                    if t == 0 and k % 2 == 0 and xp == HI:
                        pe.wait_ge((turned_hi, turned_lo)[ap], 2 * b + k // 2 + 1)
                    last = MM(slot[:, 1, t % 2, :], actT[:, 0, xp, k, t * P:(t + 1) * P], mixT[:, ap, k, :],
                              start=(n == 0), stop=(n == len(steps) - 1))
                last.then_inc(mix_done, 1)

            pe.wait_ge(ident_ready, 2)
            for n in range(WARM_UP):
                MM(sc[:, 0, 0:P], ident[:, :], ident[:, :], start=True, stop=True)
            pe.wait_ge(wqk_lo, 1)
            project(0, first=True)
            scores(0)
            project(1)

            def attend(b, projected):
                turn_attention(b)
                if not projected:
                    project(b + 1)
                mix(b, 0)
                scores(b + 1)
                for t in range(1, T):
                    mix(b, t)

            attend(0, True)
            with pe.Fori(1, B - 1) as b:
                attend(b, False)
            turn_attention(B - 1)
            mix(B - 1, 0)
            mix(B - 1, 1)
            mix(B - 1, 2)
            pe.wait_ge(normed, T)
            for k in range(T):
                last = turn(sc[:, k, :], xraw, k)
                if k % 2:
                    last.then_inc(turned, 1)
            mix(B - 1, 3)

            def gate_up_first(m, k, ap):
                MM(slot[:, 0, m, :], Whi[:, m, k * F:k * F + P], actT[:, 1, ap, k, :], start=(k == 0 and ap == HI), stop=False)

            for k in range(T):
                if k % 2 == 0:
                    pe.wait_ge(turned_hi, 2 * B + k // 2 + 1)
                gate_up_first(GATE, k, HI)
            pe.wait_ge(mix_scaled, 3)
            pe.wait_ge(odd_summed, 1)
            MM(slot[0:1, 1, 0, 0:1], oddp[:, 0:1], ones[:, 0:1], start=True, stop=True).then_inc(odd_total, 1)
            for k in range(T):
                gate_up_first(UP, k, HI)
            pe.wait_ge(out_free, 2)
            for k in (0, 1):
                for m in (GATE, UP):
                    gate_up_first(m, k, LO)

            def phase_b(general):
                parts = ((HI, HI), (HI, LO), (LO, HI))[:3 if general else 2]

                def gate_up(b, i, s, first=False):
                    c, buf = (i % NU) * P, (b + 1 + i // NU) % 2
                    if general:
                        pe.wait_ge(wlo_gu_ready, b * NU + i + 1)
                    steps = [(m, k, n) for m in (GATE, UP) for k in range(T) for n in range(len(parts))]
                    if first:
                        pe.wait_ge(out_free, T)
                        steps = [(m, k, n) for m, k, n in steps if n == 2 or (n == 1 and k >= 2)]
                    for m, k, n in steps:
                        wp, ap = parts[n]
                        w = Whi[:, m, k * F + c:k * F + c + P] if wp == HI else wlo_gu[:, (m * T + k) * P:(m * T + k + 1) * P]
                        last = MM(slot[:, s, m, :], w, actf[:, ds(buf * (2 * T * S) + (ap * T + k) * S, S)],
                                  start=(k == 0 and n == 0), stop=(k == T - 1 and n == len(parts) - 1))
                    last.then_inc(slot_ready, 1)

                def down_step(b, i, t, n):
                    wp, hp = parts[n]
                    w = Whi[:, DOWN, i * S:(i + 1) * S] if wp == HI else wlo_dn[:, 0:S]
                    step = MM(sc[:, t, :], mixT[:, hp, i % T, t * P:(t + 1) * P], w,
                              start=(i == 0 and n == 0), stop=(i == NU - 1 and n == len(parts) - 1))
                    if i == NU - 1 and n == len(parts) - 1:
                        step.then_inc(bank_done, 1)
                    return step

                def down(b, i):
                    pe.wait_ge(hid_lo, b * NU + i + 1)
                    if general:
                        pe.wait_ge(wlo_dn_ready, b * NU + i + 1)
                    for t in range(T):
                        if i == 0:
                            pe.wait_ge(out_free, b * T + t + 1)
                        for n in range(len(parts)):
                            last = down_step(b, i, t, n)
                    if i < NU - 1:
                        last.then_inc(down_done, 1)

                def downs_after(i, late):
                    if not late or i < NU - 3:
                        return [i - 1]
                    return {NU - 3: [], NU - 2: [], NU - 1: [NU - 4, NU - 3]}[i]

                def last_downs(b):
                    pe.wait_ge(hid_lo, (b + 1) * NU)
                    for t in range(T):
                        for i in (NU - 2, NU - 1):
                            for n in range(len(parts)):
                                down_step(b, i, t, n)

                def batch(b, last):
                    for kind, what, e, s in events(b, last):
                        pe.wait_ge(slot_free, e + 1)
                        if kind == "unit":
                            gate_up(b, what, s)
                            for i in downs_after(what, last and not general):
                                down(b, i)
                        else:
                            for n, k in enumerate(what):
                                if k == 0:
                                    pe.wait_ge(normed, (b + 2) * T)
                                turned_now = turn(slot[:, s, n, :], xraw, k)
                            turned_now.then_inc(slot_ready, 1)
                    if last and general:
                        down(b, NU - 1)
                    elif last:
                        last_downs(b)

                gate_up(0, 0, 0, first=True)
                pe.wait_ge(mix_scaled, T)
                with pe.Fori(0, B - 1) as b:
                    batch(b, False)
                batch(B - 1, True)

            by_weights(pe, phase_b)

        @block.scalar
        def _(act):
            A = nc.scalar.activation

            def context_hi(b):
                act.wait_ge(ctx_in, (b + 1) * DMA)
                if not isinstance(b, int) or b > 0:
                    act.wait_ge(proj_done, 2 * b)
                A(csp[:, HI, :, :], craw[:, :, :], ACT.Copy).then_inc(ctx_hi, 1)

            def project_hi(b):
                for m in (Q, K):
                    act.wait_ge(proj_done, 2 * b + m + 1)
                    A(qks[:, HI, m, :], slot[:, 0, m, :], ACT.Identity, bias=bias[:, m:m + 1]).then_inc(qk_hi, 1)

            def exp(b):
                for t in range(T):
                    act.wait_ge(max_ready, b * T + t + 1)
                    A(work[:, t, :], sc[:, t, :], ACT.Exp, bias=nmax[:, t:t + 1],
                      accum_out=rsum[:, t:t + 1]).then_inc(exp_done, 1)

            def softmax(b):
                exp(b)
                for t in range(T):
                    act.wait_ge(inv_ready, 2 * b + t // 2 + 1)
                    A(work[:, t, :], work[:, t, :], ACT.Copy, scale=rinv[:, t:t + 1]).then_inc(attn_ready, 1)

            def turned_hi_half(b, h, dst):
                act.wait_ge(turned, 2 * b + h + 1)
                A(dst[:, 2 * h:2 * h + 2, :], sc[:, 2 * h:2 * h + 2, :], ACT.Copy).then_inc(turned_hi, 1)

            def shift(b):
                act.wait_ge(scale_ready, b + 1)
                for t in range(T):
                    row = Xf[:, ds(b * (T * S) + t * S, S)]
                    A(row, row, ACT.Identity, bias=nb[:, ds(b * T + t, 1)]).then_inc(shifted, 1)

            def weights_hi(j, n):
                act.wait_ge(w_in[n], (j + 1) * DMA)
                A(Whi_flat[:, ds((j * W3 + n) * F, F)], wraw[:, n, :], ACT.Copy).then_inc(w_hi, 1)

            act.wait_ge(wqk_in, DMA)
            A(wqs[:, HI, :, :, :].rearrange("p m c d -> p (m c d)"), wqraw, ACT.Copy).then_inc(wqk_hi, 1)
            for c in range(CT):
                act.wait_ge((first_half_in, ctx_in)[c], DMA)
                A(csp[:, HI, c, :], craw[:, c, :], ACT.Copy).then_inc((first_half_hi, ctx_hi)[c], 1)
            act.wait_ge(small_in, 2 * DMA)
            A(tg[:, :], g2[:, :], ACT.Tanh).then_inc(tanh_ready, 1)
            project_hi(0)
            context_hi(1)
            exp(0)
            weights_hi(0, 0)

            def attend(b, more):
                for h in range(2):
                    turned_hi_half(b, h, mixT[:, HI])
                project_hi(b + 1)
                weights_hi(b, 1)
                shift(b)
                if more:
                    context_hi(b + 2)
                softmax(b + 1)
                weights_hi(b, 2)
                if more:
                    weights_hi(b + 1, 0)

            with act.Fori(0, B - 2) as b:
                attend(b, True)
            attend(B - 2, False)
            def scaled_mix(t):
                act.wait_ge(mix_done, (B - 1) * T + t + 1)
                A(work[:, t, :], slot[:, 1, t % 2, :], ACT.Identity, bias=nb[:, (B - 1) * T + t:(B - 1) * T + t + 1],
                  scale=s1[:, (B - 1) * T + t:(B - 1) * T + t + 1]).then_inc(mix_scaled, 1)

            for h in range(2):
                turned_hi_half(B - 1, h, mixT[:, HI])
            weights_hi(B - 1, 0)
            weights_hi(B - 1, 1)
            act.wait_ge(scale_ready, B)
            scaled_mix(0)
            weights_hi(B - 1, 2)
            scaled_mix(1)
            scaled_mix(2)
            for h in range(2):
                turned_hi_half(B, h, actT[:, 1, HI])
            scaled_mix(3)

            def phase_b(general):
                def unit(b, i, e, s):
                    act.wait_ge(slot_ready, e + 1)
                    A(craw[:, s, :], slot[:, s, GATE, :], ACT.Silu, scale=usc[:, GATE, i % NU:i % NU + 1]).then_inc(silu_done, 1)
                    act.wait_ge(slot_free, e + 3)
                    A(mixT[:, HI, (i % NU) % T, :], hid[:, s, :], ACT.Copy).then_inc(hid_hi, 1)

                def batch(b, last):
                    for kind, what, e, s in events(b, last):
                        if kind == "unit":
                            unit(b, what, e, s)
                        else:
                            act.wait_ge(slot_ready, e + 1)
                            A(actf[:, ds((b % 2) * (2 * T * S) + (HI * T + what[0]) * S, len(what) * S)],
                              slot[:, s, 0:len(what), :].rearrange("p k s -> p (k s)"), ACT.Copy).then_inc(turned_hi, 1)

                unit(0, 0, 0, 0)
                with act.Fori(0, B - 1) as b:
                    batch(b, False)
                batch(B - 1, True)

            by_weights(act, phase_b)

        @block.vector
        def _(dve):
            V = nc.vector

            def project_lo(b):
                for m in (Q, K):
                    dve.wait_ge(qk_hi, 2 * b + m + 1)
                    V.scalar_tensor_tensor(out=qks[:, LO, m, :], in0=slot[:, 0, m, :], scalar=bias[:, m:m + 1],
                                           in1=fl(qks[:, HI, m, :]), op0=ALU.add, op1=ALU.subtract).then_inc(qk_lo, 1)

            def row_stats(b, tiles, raw):
                for t in tiles:
                    V.bn_stats(st[:, t, :], Xf[:, ds(b * (T * S) + t * S, S)]).then_inc(raw, 1)

            def mean_variance(ready):
                for t in range(T):
                    last = V.bn_aggr(mv[:, t, :], st[:, t, :])
                last.then_inc(ready, 1)

            def softmax_max(b, n):
                for t in range(0, T, n):
                    dve.wait_ge(score_done, b * T + t + n)
                    V.tensor_reduce(nmax[:, t:t + n], sc[:, t:t + n, :], AX.X, ALU.max, negate=True).then_inc(max_ready, n)

            def inverse_sums(b, h):
                dve.wait_ge(exp_done, b * T + 2 * h + 2)
                V.reciprocal(rinv[:, 2 * h:2 * h + 2], rsum[:, 2 * h:2 * h + 2]).then_inc(inv_ready, 1)

            def turned_lo_half(b, h, dst, done, n):
                dve.wait_ge(turned_hi, 2 * b + h + 1)
                V.tensor_tensor(dst[:, LO, 2 * h:2 * h + 2, :], sc[:, 2 * h:2 * h + 2, :],
                                fl(dst[:, HI, 2 * h:2 * h + 2, :]), ALU.subtract).then_inc(done, n)

            def x1(b, t):
                dve.wait_ge(mix_done, b * T + t + 1)
                dve.wait_ge(shifted, b * T + t + 1)
                row = Xf[:, ds(b * (T * S) + t * S, S)]
                V.scalar_tensor_tensor(out=row, in0=slot[:, 1, t % 2, :], scalar=s1[:, ds(b * T + t, 1)],
                                       in1=row, op0=ALU.mult, op1=ALU.add).then_inc(mix_free, 1)

            def weights_check(j, n):
                dve.wait_ge(w_hi, j * W3 + n + 1)
                V.scalar_tensor_tensor(out=wraw[:, n, :], in0=wraw[:, n, :], scalar=1.0,
                                       in1=fl(Whi_flat[:, ds((j * W3 + n) * F, F)]), op0=ALU.mult, op1=ALU.not_equal,
                                       accum_out=odd[:, ds(j * W3 + n, 1)]).then_inc(w_checked, 1)

            def norm(b):
                dve.wait_ge(rstd2_ready, b + 1)
                for t in range(T):
                    V.tensor_scalar(xraw[:, t, :], Xf[:, ds(b * (T * S) + t * S, S)], mv[:, t, 0:1], rs[:, t:t + 1],
                                    ALU.subtract, ALU.mult).then_inc(normed, 1)

            dve.wait_ge(wqk_hi, 1)
            V.tensor_tensor(wqs[:, LO, :, :, :].rearrange("p m c d -> p (m c d)"), wqraw,
                            fl(wqs[:, HI, :, :, :].rearrange("p m c d -> p (m c d)")), ALU.subtract).then_inc(wqk_lo, 1)
            dve.wait_ge(first_half_hi, 1)
            dve.wait_ge(ctx_hi, 1)
            V.tensor_tensor(csp[:, LO, :, :], craw[:, :, :], fl(csp[:, HI, :, :]), ALU.subtract).then_inc(ctx_lo, 1)
            project_lo(0)
            softmax_max(0, 1)
            for h in range(2):
                inverse_sums(0, h)
                dve.wait_ge(inv_ready, h + 1)
                for t in (2 * h, 2 * h + 1):
                    V.tensor_scalar(work[:, t, :], work[:, t, :], rinv[:, t:t + 1], None, ALU.mult).then_inc(attn_ready, 1)
            dve.wait_ge(x_in, DMA)
            row_stats(0, range(T), stats_raw)
            dve.wait_ge(stats_raw, T)
            mean_variance(stats_ready)
            def attend(b):
                for h in range(2):
                    turned_lo_half(b, h, mixT, turned_lo, 1)
                project_lo(b + 1)
                weights_check(b, 0)
                dve.wait_ge(x_in, (b + 2) * DMA)
                dve.wait_ge(scale_ready, b + 1)
                row_stats(b + 1, (0,), stats_raw)
                x1(b, 0)
                row_stats(b + 1, (1,), stats_raw)
                softmax_max(b + 1, 2)
                row_stats(b + 1, (2, 3), stats_raw)
                inverse_sums(b + 1, 0)
                dve.wait_ge(stats_raw, (b + 2) * T)
                x1(b, 1)
                inverse_sums(b + 1, 1)
                mean_variance(stats_ready)
                weights_check(b, 1)
                x1(b, 2)
                weights_check(b, 2)
                x1(b, 3)

            with dve.Fori(0, B - 1) as b:
                attend(b)
            for h in range(2):
                turned_lo_half(B - 1, h, mixT, turned_lo, 1)
            dve.wait_ge(scale_ready, B)
            row_stats(0, range(T), stats2_raw)
            dve.wait_ge(stats2_raw, T)
            mean_variance(stats2_ready)
            weights_check(B - 1, 0)
            dve.wait_ge(xt_lo, B * T)
            norm(0)
            weights_check(B - 1, 1)
            turned_lo_half(B, 0, actT[:, 1], out_free, 2)
            weights_check(B - 1, 2)
            dve.wait_ge(w_checked, NP)
            V.reduce_sum(oddp[:, :], odd[:, :], AX.X).then_inc(odd_summed, 1)
            dve.wait_ge(odd_total, 1)
            V.tensor_scalar(flag[:, :], slot[0:1, 1, 0, 0:1], 0.0, None, ALU.is_gt).then_inc(flag_ready, 1)
            turned_lo_half(B, 1, actT[:, 1], out_free, 2)
            dve.wait_ge(const_in, 2 * DMA)
            V.tensor_scalar(dsb[:, :], dsb[:, :], tg[:, 1:2], None, ALU.mult).then_inc(dsb_ready, 1)

            def phase_b(general):
                def unit(b, i, e, s):
                    if not (isinstance(b, int) and b == 0 and i == 0):
                        dve.wait_ge(hid_lo, b * NU + i)
                    dve.wait_ge(silu_done, b * NU + i + 1)
                    V.scalar_tensor_tensor(out=hid[:, s, :], in0=slot[:, s, UP, :], scalar=usc[:, UP, i % NU:i % NU + 1],
                                           in1=craw[:, s, :], op0=ALU.mult, op1=ALU.mult).then_inc(slot_free, 1)
                    dve.wait_ge(hid_hi, b * NU + i + 1)
                    V.tensor_tensor(mixT[:, LO, (i % NU) % T, :], hid[:, s, :], fl(mixT[:, HI, (i % NU) % T, :]),
                                    ALU.subtract).then_inc(hid_lo, 1)

                def batch(b, last):
                    turns = 0
                    for kind, what, e, s in events(b, last):
                        if kind == "unit":
                            if what == STATS_AFTER + 1 and not last:
                                dve.wait_ge(stats2_raw, (b + 2) * T)
                            unit(b, what, e, s)
                            if what == STATS_AFTER and not last:
                                row_stats(b + 1, range(T), stats2_raw)
                            if what == STATS_AFTER + 1 and not last:
                                mean_variance(stats2_ready)
                            if what == NORM_AFTER and not last:
                                norm(b + 1)
                        else:
                            turns += 1
                            dve.wait_ge(turned_hi, 2 * (B + 1) + b * NTURN + turns)
                            at, n = (b % 2) * (2 * T * S), len(what) * S
                            V.tensor_tensor(actf[:, ds(at + (LO * T + what[0]) * S, n)],
                                            slot[:, s, 0:len(what), :].rearrange("p k s -> p (k s)"),
                                            fl(actf[:, ds(at + (HI * T + what[0]) * S, n)]), ALU.subtract).then_inc(slot_free, 1)
                    if not last:
                        for t in range(T):
                            dve.wait_ge(bank_done, b * T + t + 1)
                            V.tensor_tensor(scaled[t], sc[:, t, :], dsb[:, :], ALU.mult).then_inc(out_free, 1)
                    else:
                        dve.wait_ge(y_ready, b * T)
                        for t in range(T):
                            dve.wait_ge(bank_done, b * T + t + 1)
                            V.tensor_tensor(scaled[t], sc[:, t, :], dsb[:, :], ALU.mult).then_inc(out_free, 1)
                            if t % 2:
                                dve.wait_ge(out_free, (b + 1) * T + t + 1)
                                V.tensor_tensor(X[:, b * T + t, :], X[:, b * T + t, :], scaled[t], ALU.add).then_inc(y_last, 1)

                dve.wait_ge(x1_added, T)
                unit(0, 0, 0, 0)
                dve.wait_ge(dsb_ready, 1)
                with dve.Fori(0, B - 1) as b:
                    batch(b, False)
                batch(B - 1, True)

            by_weights(dve, phase_b)

        @block.gpsimd
        def _(pool):
            G = nc.gpsimd

            G.memset(half[:, :], -0.5)
            G.memset(zero[:, :], 0.0).then_inc(const_set, 1)
            G.memset(epst[:, :], EPS).then_inc(const_set, 1)
            G.memset(ones[:, :], 1.0).then_inc(ident_ready, 1)
            G.memset(start[:, 0:1], 0.0).then_inc(mix_free, 2)
            G.memset(start[:, 1:2], 0.0).then_inc(slot_free, 2)
            G.memset(ident[:, :], 1.0).then_inc(ident_set, 1)
            pool.wait_ge(ident_set, 1)
            G.affine_select(out=ident[:, :], in_=ident[:, :], compare_op=ALU.is_equal, fill=0.0, base=0,
                            pattern=[[-1, P]], channel_multiplier=1).then_inc(ident_ready, 1)

            def split_x(b, t):
                cols = slice(t * P, (t + 1) * P)
                G.tensor_tensor(actT[:, 0, HI, :, cols], xraw[:, :, cols],
                                zero[:, 0:1].unsqueeze(1).to_broadcast([P, T, P]), ALU.add).then_inc(xt_hi, 1)
                pool.wait_ge(xt_hi, b * T + t + 1)
                G.tensor_tensor(actT[:, 0, LO, :, cols], xraw[:, :, cols], fl(actT[:, 0, HI, :, cols]),
                                ALU.subtract).then_inc(xt_lo, 1)

            def context_lo(b):
                pool.wait_ge(ctx_hi, b + 1)
                G.tensor_tensor(csp[:, LO, :, :], craw[:, :, :], fl(csp[:, HI, :, :]), ALU.subtract).then_inc(ctx_lo, 1)

            def rstd(step):
                G.tensor_tensor(ve[:, :], mv[:, :, 1], epst[:, :], ALU.add).then_inc(pool_step, 1)
                pool.wait_ge(pool_step, step)
                return G.tensor_tensor(rs[:, :], ve[:, :], half[:, :], ALU.pow)

            def scale_x(b):
                pool.wait_ge(stats_ready, b + 1)
                rstd(2 * b + 1).then_inc(pool_step, 1)
                G.tensor_scalar(ms[:, :], mv[:, :, 0], -1.0, None, ALU.mult)
                pool.wait_ge(pool_step, 2 * b + 2)
                G.tensor_tensor(s1[:, ds(b * T, T)], rs[:, :], tg[:, 0:1].to_broadcast([P, T]), ALU.mult).then_inc(xt_scaled, 1)
                pool.wait_ge(xt_scaled, b + 1)
                G.tensor_tensor(nb[:, ds(b * T, T)], ms[:, :], s1[:, ds(b * T, T)], ALU.mult).then_inc(scale_ready, 1)

            pool.wait_ge(const_set, 2)
            pool.wait_ge(xt_in, DMA)
            split_x(0, 0)
            context_lo(1)
            split_x(0, 1)
            split_x(0, 2)
            split_x(0, 3)
            pool.wait_ge(tanh_ready, 1)
            scale_x(0)

            def attend(b, more2):
                pool.wait_ge(xt_in, (b + 2) * DMA)
                for t in range(T):
                    pool.wait_ge(mix_done, b * T + t + 1)
                    split_x(b + 1, t)
                    if t == 0:
                        if more2:
                            context_lo(b + 2)
                        scale_x(b + 1)

            with pool.Fori(0, B - 2) as b:
                attend(b, True)
            attend(B - 2, False)

            def rstd2(b):
                pool.wait_ge(stats2_ready, b + 1)
                rstd(2 * B + b + 1).then_inc(rstd2_ready, 1)

            rstd2(0)
            for t in range(T):
                pool.wait_ge(mix_scaled, t + 1)
                row = X[:, (B - 1) * T + t, :]
                G.tensor_tensor(row, row, work[:, t, :], ALU.add).then_inc(x1_added, 1)

            def phase_b(general):
                def low_weights(b, i):
                    u, c = b * NU + i, (i % NU) * P
                    pool.wait_ge(raw_in, (u + 1) * (2 + T) * DMA)
                    if not isinstance(b, int) or u > 0:
                        pool.wait_ge(silu_done, u)
                    for m in (GATE, UP):
                        last = G.tensor_tensor(wlo_gu[:, m * T * P:(m + 1) * T * P].rearrange("p (k c) -> p k c", c=P),
                                               wraw[:, m, 0:T * P].rearrange("p (k c) -> p k c", c=P),
                                               fl(Whi[:, m, :]).rearrange("p (k f) -> p k f", f=F)[:, :, c:c + P], ALU.subtract)
                    last.then_inc(wlo_gu_ready, 1)
                    if i == NU:
                        pool.wait_ge(bank_done, (b + 1) * T)
                    elif i > 0:
                        pool.wait_ge(down_done, b * (NU - 1) + i)
                    G.tensor_tensor(wlo_dn[:, 0:S], wraw[:, DOWN, 0:S], fl(Whi[:, DOWN, (i % NU) * S:(i % NU + 1) * S]),
                                    ALU.subtract).then_inc(wlo_dn_ready, 1)

                def batch(b, last):
                    for kind, what, e, s in events(b, last):
                        if kind == "unit":
                            if general:
                                low_weights(b, what)
                            if what == STATS_AFTER + 2 and not last:
                                rstd2(b + 1)
                    for t in (0, 2) if last else range(T):
                        pool.wait_ge(out_free, (b + 1) * T + t + 1)
                        row = Xf[:, ds(b * (T * S) + t * S, S)]
                        G.tensor_tensor(row, row, scaled[t], ALU.add).then_inc(y_ready, 1)

                if general:
                    low_weights(0, 0)
                with pool.Fori(0, B - 1) as b:
                    batch(b, False)
                batch(B - 1, True)

            by_weights(pool, phase_b)


def kernel(**inputs):
    import numpy as np
    import concourse.bacc as bacc
    from concourse.bass_utils import run_bass_kernel_spmd

    a = {k: np.asarray(v) for k, v in inputs.items()}

    def rows(w, tiles):
        return w.reshape(tiles, P, -1).transpose(1, 0, 2).reshape(P, -1)

    arrays = {
        "x": a["x"],
        "xT": a["x"].transpose(0, 2, 1),
        "ctxT": a["ctx_1024"].transpose(0, 2, 1),
        "wqk": np.stack([a["L0_xattn_Wq"].T, a["L0_xattn_Wk"].T]),
        "bqk": np.stack([a["L0_xattn_bq"], a["L0_xattn_bk"]], axis=1),
        "gates": np.concatenate([a["g_xattn"], a["g_ffn"]]),
        "w3": np.concatenate([rows(a[f"L0_ffn_{w}_w"].T, n).reshape(P, T, F).transpose(1, 0, 2)
                              for w, n in (("gate", T), ("up", T), ("down", NU))]),
        "scales": np.concatenate([a["L0_ffn_gate_s"].reshape(NU, P).T, a["L0_ffn_up_s"].reshape(NU, P).T], axis=1),
        "down_s": a["L0_ffn_down_s"],
    }
    arrays = {k: np.ascontiguousarray(v) for k, v in arrays.items()}
    nc = bacc.Bacc("TRN2", target_bir_lowering=False, num_devices=1)
    args = [nc.dram_tensor(k, v.shape, mybir.dt.from_np(v.dtype), kind="ExternalInput").ap() for k, v in arrays.items()]
    out = nc.dram_tensor("out", (B, S, S), mybir.dt.float32, kind="ExternalOutput").ap()
    flamingo_kernel(nc, *args, out)
    return run_bass_kernel_spmd(nc, [arrays], core_ids=[0]).results[0]["out"]
```
